# Optimizing a Trainium2 kernel written in Bass

```python
import numpy as np
import jax
import jax.numpy as jnp

def _softmax(x, axis=-1):
    return jax.nn.softmax(x, axis=axis)
def _gelu(x):
    return jax.nn.gelu(x, approximate=True)
def _silu(x):
    return jax.nn.silu(x)
def _sigmoid(x):
    return jax.nn.sigmoid(x)
def _layernorm(x, axis=-1, eps=1e-5):
    m = jnp.mean(x, axis=axis, keepdims=True)
    v = jnp.var(x, axis=axis, keepdims=True)
    return (x - m) / jnp.sqrt(v + eps)
def _scatter_add(tgt, idx, src, axis=0):
    return tgt.at[idx].add(src)
def _segment_sum(src, seg, n):
    return jax.ops.segment_sum(src, seg, n)

kernel_name = 'mk_conv_preact_d2_conv_nhwc768_28efdd'

def setup_inputs(seed: int = 0):
    np.random.seed(seed)
    _w = jnp.asarray
    def _rec_inputs():
        import jax
        import jax.numpy as jnp
        _gk = jax.random.key(seed)
        x = -0.0005963 + 1.001 * jax.random.normal(jax.random.fold_in(_gk, 1), (4, 32, 32, 768), jnp.float32)
        return x
    x = _rec_inputs()
    def _L0_conv_setup():
        import jax, jax.numpy as jnp
        import numpy as np
        NUM_HEADS = 12

        def _get_rel_pos(size: int, rel_pos: jnp.ndarray) -> jnp.ndarray:
            coords = jnp.arange(size)[:, None] - jnp.arange(size)[None, :] + (size - 1)
            return rel_pos[coords]
        key = jax.random.key(seed)
        ks = jax.random.split(key, 6)
        C = 768
        hd = C // NUM_HEADS
        H = W = 32
        x = jax.random.normal(ks[0], (4, H, W, C), dtype=jnp.float32)
        Wqkv = jax.random.normal(ks[1], (C, 3 * C), dtype=jnp.float32) * 0.02
        Wproj = jax.random.normal(ks[2], (C, C), dtype=jnp.float32) * 0.02
        bproj = jax.random.normal(ks[3], (C,), dtype=jnp.float32) * 0.02
        rel_pos_h = jax.random.normal(ks[4], (2 * H - 1, hd), dtype=jnp.float32) * 0.02
        rel_pos_w = jax.random.normal(ks[5], (2 * W - 1, hd), dtype=jnp.float32) * 0.02
        return {'x': x, 'Wqkv': Wqkv, 'Wproj': Wproj, 'bproj': bproj, 'rel_pos_h': rel_pos_h, 'rel_pos_w': rel_pos_w}
    _L0_conv_all = _L0_conv_setup()
    _L0_conv_in = {k: v for k, v in _L0_conv_all.items() if k in ('Wqkv', 'Wproj', 'bproj', 'rel_pos_h', 'rel_pos_w', )}
    del _L0_conv_all

    def _L1_conv_setup():
        import jax, jax.numpy as jnp
        import numpy as np
        NUM_HEADS = 12

        def _rel_gather(rel_pos, size):
            coords = jnp.arange(size)[:, None] - jnp.arange(size)[None, :] + (size - 1)
            return rel_pos[coords]
        key = jax.random.key(seed)
        ks = jax.random.split(key, 7)
        B, H, W, C = (1, 48, 48, 768)
        hd = C // NUM_HEADS
        s = 0.02
        return {'x': jax.random.normal(ks[0], (B, H, W, C), jnp.float32), 'qkv_w': jax.random.normal(ks[1], (C, 3 * C), jnp.float32) * s, 'qkv_b': jax.random.normal(ks[2], (3 * C,), jnp.float32) * s, 'proj_w': jax.random.normal(ks[3], (C, C), jnp.float32) * s, 'proj_b': jax.random.normal(ks[4], (C,), jnp.float32) * s, 'rel_pos_h': jax.random.normal(ks[5], (2 * H - 1, hd), jnp.float32) * s, 'rel_pos_w': jax.random.normal(ks[6], (2 * W - 1, hd), jnp.float32) * s}
    _L1_conv_all = _L1_conv_setup()
    _L1_conv_in = {k: v for k, v in _L1_conv_all.items() if k in ('qkv_w', 'qkv_b', 'proj_w', 'proj_b', 'rel_pos_h', 'rel_pos_w', )}
    del _L1_conv_all

    return {
        "x": x,
        "L0_conv_Wqkv": _L0_conv_in["Wqkv"],
        "L0_conv_Wproj": _L0_conv_in["Wproj"],
        "L0_conv_bproj": _L0_conv_in["bproj"],
        "L0_conv_rel_pos_h": _L0_conv_in["rel_pos_h"],
        "L0_conv_rel_pos_w": _L0_conv_in["rel_pos_w"],
        "L1_conv_qkv_w": _L1_conv_in["qkv_w"],
        "L1_conv_qkv_b": _L1_conv_in["qkv_b"],
        "L1_conv_proj_w": _L1_conv_in["proj_w"],
        "L1_conv_proj_b": _L1_conv_in["proj_b"],
        "L1_conv_rel_pos_h": _L1_conv_in["rel_pos_h"],
        "L1_conv_rel_pos_w": _L1_conv_in["rel_pos_w"],
    }

def reference(x, L0_conv_Wqkv, L0_conv_Wproj, L0_conv_bproj, L0_conv_rel_pos_h, L0_conv_rel_pos_w, L1_conv_qkv_w, L1_conv_qkv_b, L1_conv_proj_w, L1_conv_proj_b, L1_conv_rel_pos_h, L1_conv_rel_pos_w):
    import jax
    import jax.numpy as jnp
    def _L0_conv_ref(x, Wqkv, Wproj, bproj, rel_pos_h, rel_pos_w):
        import jax, jax.numpy as jnp
        import numpy as np
        NUM_HEADS = 12

        def _get_rel_pos(size: int, rel_pos: jnp.ndarray) -> jnp.ndarray:
            coords = jnp.arange(size)[:, None] - jnp.arange(size)[None, :] + (size - 1)
            return rel_pos[coords]
        B, H, W, C = x.shape
        hn = NUM_HEADS
        hd = C // hn
        scale = hd ** (-0.5)
        S = H * W
        qkv = x @ Wqkv
        qkv = qkv.reshape(B, S, 3, hn, hd)
        qkv = jnp.transpose(qkv, (2, 0, 3, 1, 4)).reshape(3, B * hn, S, hd)
        q, k, v = (qkv[0], qkv[1], qkv[2])
        Rh = _get_rel_pos(H, rel_pos_h)
        Rw = _get_rel_pos(W, rel_pos_w)
        r_q = q.reshape(B * hn, H, W, hd)
        rel_h = jnp.einsum('bhwc,hkc->bhwk', r_q, Rh)
        rel_w = jnp.einsum('bhwc,wkc->bhwk', r_q, Rw)
        bias = rel_h[..., :, None] + rel_w[..., None, :]
        bias = bias.reshape(B * hn, S, S)
        scores = scale * jnp.einsum('bqc,bkc->bqk', q, k) + bias
        attn = jax.nn.softmax(scores, axis=-1)
        out = jnp.einsum('bqk,bkc->bqc', attn, v)
        out = out.reshape(B, hn, H, W, hd)
        out = jnp.transpose(out, (0, 2, 3, 1, 4)).reshape(B, H, W, C)
        return out @ Wproj + bproj

    def _L1_conv_ref(x, qkv_w, qkv_b, proj_w, proj_b, rel_pos_h, rel_pos_w):
        import jax, jax.numpy as jnp
        import numpy as np
        NUM_HEADS = 12

        def _rel_gather(rel_pos, size):
            coords = jnp.arange(size)[:, None] - jnp.arange(size)[None, :] + (size - 1)
            return rel_pos[coords]
        B, H, W, C = x.shape
        nh = NUM_HEADS
        hd = C // nh
        scale = hd ** (-0.5)
        S = H * W
        qkv = x @ qkv_w + qkv_b
        qkv = qkv.reshape(B, S, 3, nh, hd).transpose(2, 0, 3, 1, 4)
        qkv = qkv.reshape(3, B * nh, S, hd)
        q, k, v = (qkv[0], qkv[1], qkv[2])
        attn = jnp.einsum('bqd,bkd->bqk', q * scale, k)
        Rh = _rel_gather(rel_pos_h, H)
        Rw = _rel_gather(rel_pos_w, W)
        qr = q.reshape(B * nh, H, W, hd)
        rel_h = jnp.einsum('bhwc,hkc->bhwk', qr, Rh)
        rel_w = jnp.einsum('bhwc,wkc->bhwk', qr, Rw)
        bias = (rel_h[..., :, None] + rel_w[..., None, :]).reshape(B * nh, S, S)
        attn = jax.nn.softmax(attn + bias, axis=-1)
        out = jnp.einsum('bqk,bkd->bqd', attn, v)
        out = out.reshape(B, nh, H, W, hd).transpose(0, 2, 3, 1, 4).reshape(B, H, W, C)
        return out @ proj_w + proj_b

    def _gn(v, G=32, eps=1e-5):
        B_, H_, W_, C_ = v.shape
        g = v.reshape(B_, H_, W_, G, C_ // G)
        m = jnp.mean(g, axis=(1, 2, 4), keepdims=True)
        s = jnp.var(g, axis=(1, 2, 4), keepdims=True)
        return ((g - m) / jnp.sqrt(s + eps)).reshape(v.shape)

    def _ln_c(v, eps=1e-6):
        m = jnp.mean(v, axis=-1, keepdims=True)
        s = jnp.var(v, axis=-1, keepdims=True)
        return (v - m) / jnp.sqrt(s + eps)

    def _ln_t(v, eps=1e-5):
        m = jnp.mean(v, axis=-1, keepdims=True)
        s = jnp.var(v, axis=-1, keepdims=True)
        return (v - m) / jnp.sqrt(s + eps)

    def _to_tokens(v):
        B_, H_, W_, C_ = v.shape
        return v.reshape(B_, H_ * W_, C_)
    def _from_tokens(t, like):
        return t.reshape(like.shape)

    x = x + _L0_conv_ref(_gn(x), L0_conv_Wqkv, L0_conv_Wproj, L0_conv_bproj, L0_conv_rel_pos_h, L0_conv_rel_pos_w)
    x = x + _L1_conv_ref(_gn(x), L1_conv_qkv_w, L1_conv_qkv_b, L1_conv_proj_w, L1_conv_proj_b, L1_conv_rel_pos_h, L1_conv_rel_pos_w)
    return x


_drawn_inputs = setup_inputs


def setup_inputs(seed=0):
    import zlib

    import numpy as np

    out = dict(_drawn_inputs(seed))
    spreads = {}
    factors = {'L0_conv_Wqkv': 5.193,
     'L0_conv_Wproj': 5.242,
     'L0_conv_bproj': 11.743,
     'L0_conv_rel_pos_h': 8.0,
     'L0_conv_rel_pos_w': 8.0,
     'L1_conv_qkv_w': 4.572,
     'L1_conv_qkv_b': 5.339,
     'L1_conv_proj_w': 3.364,
     'L1_conv_proj_b': 21.865,
     'L1_conv_rel_pos_h': 8.0,
     'L1_conv_rel_pos_w': 8.0}
    for name, (base, spread) in spreads.items():
        noise = np.random.default_rng([zlib.crc32(name.encode()), seed]).standard_normal(out[name].shape)
        drawn = base * np.exp(spread * noise) if base else spread * noise
        out[name] = jnp.asarray(drawn.astype(out[name].dtype))
    for name, factor in factors.items():
        out[name] = (out[name] * factor).astype(out[name].dtype)
    return out
```

```python
from contextlib import ExitStack

import concourse.bass as bass
from concourse import mybir

F32 = mybir.dt.float32
F32R = mybir.dt.float32r
ALU = mybir.AluOpType
ACT = mybir.ActivationFunctionType
AX_X = mybir.AxisListType.X

P = 128
LAYERS, B, HW, C = 2, 4, 32, 768
S = HW * HW
HEADS, HD = 12, 64
PAIRS = HEADS // 2
CT = C // P
TT = S // P
GROUPS = 32
HALF = 512
WC = 256
QKV_CHUNKS, PROJ_CHUNKS = 3 * C // WC, C // WC
CHUNKS = QKV_CHUNKS + PROJ_CHUNKS
OFFS = 2 * HW - 1
SCALE = HD ** -0.5
EPS = 1e-5
STEPS = 8
AHEAD = 2
MAX_AT = {6: [0], 7: [1], 0: [2], 1: [3], 2: [4], 3: [5, 6], 4: [7]}
ROW_AT = 5
MAX_FIRST = (3, 4)


def two_layers(nc, x, wqkv, wproj, qk_bias, v_bias, proj_bias, rel, onehot, ident, member, member_t,
               state):
    with ExitStack() as ctx:
        def sb(name, shape, dt=F32):
            return ctx.enter_context(nc.sbuf_tensor(name, shape, dt))

        def sem(name):
            return ctx.enter_context(nc.semaphore(name))

        sums_dram = nc.dram_tensor("sums_scratch", (LAYERS * B, HEADS, S), F32, kind="Internal").ap()
        recips_dram = nc.dram_tensor("recips_scratch", (LAYERS * B, HEADS, S), F32, kind="Internal").ap()

        qa = [sb("q_even", [P, CT, S]), sb("q_odd", [P, CT, S])]
        xT = qa[0]
        attn = qa[0]
        k32 = sb("k32", [P, CT, S])
        recip = k32
        v32 = sb("v32", [P, TT, C])
        xin = v32
        qT = v32[:, :, :].rearrange("p t c -> p (t c)").rearrange("p (m s) -> p m s", m=CT)
        wraw = sb("wraw", [P, 2, CT, WC])
        p32 = wraw[:, :, :, :].rearrange("p a k n -> p (a k n)")[:, 0:2 * S].rearrange("p (a n) -> p a n", a=2)
        sumrow = sb("sumrow", [P, S])
        hot = sb("hot", [P, S])
        idt = sb("idt", [P, P])
        tab = sb("tab", [P, 2, OFFS])
        qkb = sb("qkb", [P, 2 * CT])
        rowb = sb("rowb", [P, C])
        memb = sb("memb", [P, CT, GROUPS])
        membt = sb("membt", [GROUPS, CT, P])
        stats = sb("stats", [P, CT, 12])
        mv = sb("mv", [P, CT, 2])
        gstat = sb("gstat", [GROUPS, 4])
        cmean = sb("cmean", [P, CT])
        crstd = sb("crstd", [P, CT])
        dev = sb("dev", [P, CT])
        dev2 = sb("dev2", [P, CT])
        cvar = sb("cvar", [P, CT])
        nmax = sb("nmax", [P, 2, TT])
        rs = sb("rs", [P, HEADS * S // P])

        k32_flat = k32[:, :, :].rearrange("p m s -> p (m s)")
        by_row = k32_flat[:, 0:HW * 96].rearrange("p (a n) -> p a n", n=96)
        by_col = [k32_flat[:, HW * 96:].rearrange("p (a n) -> p a n", n=P),
                  sumrow[:, :].rearrange("p (a n) -> p a n", n=P)]

        def windows(e, kind, first, count):
            base = tab[own[e], kind, first:first + 1]
            return bass.AP(tensor=base.tensor, offset=base.offset, ap=[list(base.ap[0]), [1, count], [1, HW]])

        R = sb("R", [P, 18 * S], F32R)
        xh = R[:, 0:CT * S].rearrange("p (k s) -> p k s", k=CT)
        xl = R[:, CT * S:2 * CT * S].rearrange("p (k s) -> p k s", k=CT)

        def wsplit(slot, low):
            o = 2 * CT * S + (2 * slot + low) * CT * WC
            return R[:, o:o + CT * WC].rearrange("p (k n) -> p k n", k=CT)

        def rtile(i):
            return R[:, i * S:(i + 1) * S]

        Qh, Ql, Q3, Kh, K3 = ([rtile(7 * e + i) for e in range(2)] for i in range(5))
        V1, V0 = ([rtile(7 * e + i).rearrange("p (t m) -> p t m", t=TT) for e in range(2)] for i in (5, 6))
        Ph = [rtile(14), rtile(15)]
        Pl = [rtile(16), rtile(17)]
        own = [slice(0, HD), slice(HD, P)]
        other = [slice(HD, P), slice(0, HD)]
        first_other = [HD, 0]

        ps = ctx.enter_context(nc.psum_tensor("ps", [P, 8, HALF], F32))

        def D(i):
            return ps[:, 2 * i:2 * i + 2, :].rearrange("p a n -> p (a n)")

        consts = sem("consts")
        small = sem("small")
        rowb_loaded = sem("rowb_loaded")
        x_loaded = sem("x_loaded")
        resid_loaded = sem("resid_loaded")
        copied = sem("copied")
        w_loaded = [sem("w_loaded0"), sem("w_loaded1")]
        primed = sem("primed")
        gate = sem("gate")
        tab_zero = sem("tab_zero")
        tab_ready = sem("tab_ready")
        tr_done = sem("tr_done")
        xt_ready = sem("xt_ready")
        stat_ready = sem("stat_ready")
        aggr_ready = sem("aggr_ready")
        norm_pe = sem("norm_pe")
        norm_dve = sem("norm_dve")
        norm_pool = sem("norm_pool")
        xn_ready = sem("xn_ready")
        xh_ready = sem("xh_ready")
        xs_ready = sem("xs_ready")
        wh_ready = sem("wh_ready")
        ws_ready = sem("ws_ready")
        mt_done = sem("mt_done")
        mt_act = sem("mt_act")
        mt_dve = sem("mt_dve")
        rel_done = sem("rel_done")
        rel_act = sem("rel_act")
        rel_dve = sem("rel_dve")
        v_done = sem("v_done")
        v_evac = sem("v_evac")
        fill_dve = sem("fill_dve")
        qh_ready = sem("qh_ready")
        kh_ready = sem("kh_ready")
        q3_ready = sem("q3_ready")
        low_ready = sem("low_ready")
        v1_ready = sem("v1_ready")
        v0_ready = sem("v0_ready")
        max_done = sem("max_done")
        max_taken = sem("max_taken")
        row_done = sem("row_done")
        row_ready = sem("row_ready")
        sc_done = sem("sc_done")
        probs_ready = sem("probs_ready")
        lo_ready = sem("lo_ready")
        pv_done = sem("pv_done")
        out_taken = sem("out_taken")
        sum_taken = sem("sum_taken")
        sum_stored = [sem("sum_stored0"), sem("sum_stored1")]
        rs_loaded = sem("rs_loaded")
        rs_ready = sem("rs_ready")
        rs_stored = sem("rs_stored")
        recip_loaded = sem("recip_loaded")
        an_ready = sem("an_ready")
        ah_ready = sem("ah_ready")
        as_ready = sem("as_ready")
        xb_ready = sem("xb_ready")
        y_done = sem("y_done")
        y_evac = sem("y_evac")
        stored = sem("stored")

        block = ctx.enter_context(nc.Block())

        def rel_out(op, ps, dst, r, base, on_act):
            at = 2 * (r % (HW // 2))
            by_row = r < HW // 2
            q = base + (0 if by_row else HW)
            grid = dst[q:q + HW, :, :].rearrange("p m (h w) -> p m h w", h=HW)
            if by_row:
                out = grid[:, :, at:at + 2, :].rearrange("p m a w -> p a m w")
            else:
                out = grid[:, :, :, at:at + 2].rearrange("p m h a -> p a m h")
            in_ = ps[q:q + HW, r % 8, 0:2 * CT * HW].rearrange("p (a m w) -> p a m w", a=2, m=CT)
            return op(out, in_, ACT.Copy) if on_act else op(out, in_)

        @block.sync
        def _(sp):
            for dst, src in ((idt, ident), (hot, onehot), (memb, member), (membt, member_t)):
                sp.dma_start(dst[tuple([slice(None)] * len(dst.shape))], src).then_inc(consts, 16)
            sp.dma_start(xin[:, :, :], x[0].rearrange("(t p) c -> p t c", p=P)).then_inc(x_loaded, 16)
            sp.dma_start(state[0:B], x).then_inc(copied, 16)

            def load_chunk(lb, layer, j):
                sp.wait_ge(ws_ready, CHUNKS * lb + j + 1)
                sp.sem_inc(gate, 1)
                w, c0 = (wqkv, j * WC) if j < QKV_CHUNKS else (wproj, (j - QKV_CHUNKS) * WC)
                src = w[bass.ds(layer, 1), :, c0:c0 + WC].rearrange("a (k p) n -> p (a k) n", p=P)
                sp.dma_start(wraw[:, j % 2, :, :], src).then_inc(w_loaded[j % 2], 16)

            with sp.Fori(0, LAYERS * B) as lb:
                layer = lb // B
                sp.dma_start(tab[:, :, :], rel[bass.ds(layer, 1)].rearrange("a p r n -> p (a r) n")).then_inc(small, 16)
                sp.dma_start(qkb[:, :], qk_bias[bass.ds(layer, 1)].rearrange("a p m -> p (a m)")).then_inc(small, 16)
                sp.dma_start(rowb[:, :], v_bias[bass.ds(layer, 1)].to_broadcast([P, C])).then_inc(rowb_loaded, 16)
                for j in range(QKV_CHUNKS):
                    load_chunk(lb, layer, j)
                sp.wait_ge(v_evac, CT * (lb + 1))
                sp.sem_inc(gate, 1)
                sp.dma_start(rowb[:, :], proj_bias[bass.ds(layer, 1)].to_broadcast([P, C])).then_inc(rowb_loaded, 16)

                with sp.Fori(0, PAIRS) as p:
                    for e in range(2):
                        sp.wait_ge(sum_taken, 2 * (2 * (PAIRS * lb + p) + e) + 4)
                        sp.sem_inc(gate, 1)
                        r = first_other[e]
                        sp.dma_start(sums_dram[bass.ds(lb, 1), bass.ds(2 * p + e, 1), :].rearrange("a h s -> (a h) s"),
                                     sumrow[r:r + 1, :]).then_inc(sum_stored[e], 16)
                sp.wait_ge(v0_ready, HEADS * (lb + 1))
                sp.sem_inc(gate, 1)
                sp.wait_ge(copied, 16)
                sp.sem_inc(gate, 1)
                sp.dma_start(xin[:, :, :], state[bass.ds(lb, 1)].rearrange("a (t p) c -> p (a t) c", p=P)).then_inc(resid_loaded, 16)
                for e in range(2):
                    sp.wait_ge(sum_stored[e], 16 * PAIRS * (lb + 1) + 16)
                    sp.sem_inc(gate, 1)
                sp.dma_start(rs[:, :], sums_dram[bass.ds(lb, 1)].rearrange("a h s -> (a h s)").rearrange("(p n) -> p n", p=P)).then_inc(rs_loaded, 16)
                sp.wait_ge(lo_ready, 2 * S // P * PAIRS * (lb + 1) + 2)
                sp.sem_inc(gate, 1)
                load_chunk(lb, layer, QKV_CHUNKS)
                load_chunk(lb, layer, QKV_CHUNKS + 1)
                sp.wait_ge(rs_ready, lb + 1)
                sp.sem_inc(gate, 1)
                sp.dma_start(recips_dram[bass.ds(lb, 1)].rearrange("a h s -> (a h s)").rearrange("(p n) -> p n", p=P), rs[:, :]).then_inc(rs_stored, 16)
                sp.wait_ge(rs_stored, 16 * (lb + 1))
                sp.sem_inc(gate, 1)
                for e in range(2):
                    src = recips_dram[bass.ds(lb, 1)].rearrange("a (p e) s -> a e p s", e=2)[:, e].to_broadcast([HD, PAIRS, S])
                    sp.dma_start(recip[own[e], :, :], src).then_inc(recip_loaded, 16)
                load_chunk(lb, layer, QKV_CHUNKS + 2)
                sp.wait_ge(y_evac, CT * (lb + 1) + 1)
                sp.sem_inc(gate, 1)
                sp.dma_start(state[bass.ds(lb + B, 1)].rearrange("a (t p) c -> p (a t) c", p=P), xin[:, :, :]).then_inc(stored, 16)
                sp.wait_ge(stored, 16 * (lb + 1))
                sp.sem_inc(gate, 1)
                sp.dma_start(xin[:, :, :], state[bass.ds(lb + 1, 1)].rearrange("a (t p) c -> p (a t) c", p=P)).then_inc(x_loaded, 16)
            sp.wait_ge(x_loaded, 16 * (LAYERS * B + 1))
            sp.sem_inc(gate, 1)

        @block.tensor
        def _(pe):
            def three(out, a, b, first, last, width_ok=True):
                pe.matmul(out, a[0], b[0], start=first, stop=False)
                pe.matmul(out, a[0], b[1], start=False, stop=False)
                return pe.matmul(out, a[1], b[0], start=False, stop=last)

            def transposed_weights_tile(slot, m, dst):
                cols = slice(m * P, (m + 1) * P)
                for half in range(2):
                    toks = slice(half * HALF, (half + 1) * HALF)
                    for k in range(CT):
                        last = three(dst[:, toks], (wsplit(slot, 0)[:, k, cols], wsplit(slot, 1)[:, k, cols]),
                                     (xh[:, k, toks], xl[:, k, toks]), k == 0, k == CT - 1)
                return last

            def token_tile(slot, t, dst):
                toks = slice(t * P, (t + 1) * P)
                for k in range(CT):
                    last = three(dst, (xh[:, k, toks], xl[:, k, toks]),
                                 (wsplit(slot, 0)[:, k, :], wsplit(slot, 1)[:, k, :]), k == 0, k == CT - 1)
                return last

            def max_tile(e, n, j, guarded=True):
                if j == 0:
                    pe.wait_ge(qh_ready, n + 1)
                    pe.wait_ge(kh_ready, n + 1)
                    if guarded:
                        pe.wait_ge(row_ready, n)
                else:
                    pe.wait_ge(max_taken, STEPS * n + j)
                for half in range(2):
                    ks = slice(half * HALF, (half + 1) * HALF)
                    last = pe.matmul(D(2)[:, ks], Qh[e][:, j * P:(j + 1) * P], Kh[e][:, ks], start=True, stop=True)
                last.then_inc(max_done, 1)

            def max_row(e, n):
                pe.wait_ge(max_taken, STEPS * (n + 1))
                for j in range(TT):
                    last = pe.matmul(D(2)[0:1, j * P:(j + 1) * P], nmax[:, e, j:j + 1], idt[:, :], start=True, stop=True)
                last.then_inc(row_done, 1)

            def scores(e, n, u, s, guarded=True):
                if u == 0:
                    pe.wait_ge(low_ready, 2 * (n + 1))
                    pe.wait_ge(q3_ready, n + 1)
                    pe.wait_ge(row_ready, n + 1)
                if guarded:
                    pe.wait_ge(probs_ready, 2 * s - 2)
                qs = slice(u // 4 * HALF, (u // 4 + 1) * HALF)
                for i in range(2):
                    kt = 2 * (u % 4) + i
                    ks = slice(kt * P, (kt + 1) * P)
                    out = D(u % 2)[:, i * HALF:(i + 1) * HALF]
                    pe.matmul(out, K3[e][:, ks], Q3[e][:, qs], start=True, stop=False)
                    pe.matmul(out, Kh[e][:, ks], Ql[e][:, qs], start=False, stop=False)
                    last = pe.matmul(out, Kh[e][:, ks], Qh[e][:, qs], start=False, stop=True)
                last.then_inc(sc_done, 1)

            def values(e, n, u, s):
                half = u // 4
                if u == 0:
                    pe.wait_ge(v0_ready, n + 1)
                if u % 4 == 0:
                    pe.wait_ge(out_taken, 2 * n + half + 1)
                    pe.wait_ge(sum_taken, 2 * n + half + 1)
                pe.wait_ge(lo_ready, s + 3)
                out = ps[:, 6 + half, :]
                for i in range(2):
                    kt = 2 * (u % 4) + i
                    cols = slice(i * HALF, (i + 1) * HALF)
                    pe.matmul(out, V1[e][:, kt, :], Pl[u % 2][:, cols], start=(u % 4 == 0 and i == 0), stop=False)
                    pe.matmul(out, V0[e][:, kt, :], Ph[u % 2][:, cols], start=False, stop=False)
                    last = pe.matmul(out, V1[e][:, kt, :], Ph[u % 2][:, cols], start=False, stop=(u % 4 == 3 and i == 1))
                last.then_inc(pv_done, 1)

            def pair(g, last_pair):
                for t in range(2 * STEPS):
                    e, u = t // STEPS, t % STEPS
                    n, s = 2 * g + e, 2 * STEPS * g + t
                    following = not (last_pair and e == 1)
                    if u == ROW_AT and following:
                        max_row(1 - e, n + 1)
                    if not (last_pair and t + AHEAD >= 2 * STEPS):
                        e2, u2 = (t + AHEAD) // STEPS % 2, (t + AHEAD) % STEPS
                        scores(e2, 2 * g + (t + AHEAD) // STEPS, u2, s + AHEAD)
                    tiles = MAX_AT.get(u, [])
                    ahead = 2 if u > ROW_AT else 1
                    if last_pair and e + ahead > 1:
                        tiles = []
                    early = tiles[:1] if u in MAX_FIRST else []
                    for j in early:
                        max_tile((e + ahead) % 2, n + ahead, j)
                    values(e, n, u, s)
                    for j in tiles[len(early):]:
                        max_tile((e + ahead) % 2, n + ahead, j)

            pe.wait_ge(consts, 64)
            with pe.Fori(0, LAYERS * B) as lb:
                pe.wait_ge(x_loaded, 16 * (lb + 1))
                pe.wait_ge(y_evac, CT * lb + 1)
                for c in range(CT):
                    if c >= 4:
                        pe.wait_ge(xt_ready, CT * lb + c - 3)
                    for t in range(TT):
                        last = pe.transpose(D(c % 4)[:, t * P:(t + 1) * P], xin[:, t, c * P:(c + 1) * P], idt[:, :])
                    last.then_inc(tr_done, 1)
                pe.wait_ge(xt_ready, CT * (lb + 1))
                pe.wait_ge(aggr_ready, CT * (lb + 1))
                for c in range(CT):
                    last = pe.matmul(ps[0:GROUPS, 0, 0:1], memb[:, c, :], mv[:, c, 0:1], start=(c == 0), stop=(c == CT - 1))
                last.then_inc(norm_pe, 1)
                pe.wait_ge(norm_dve, 7 * lb + 1)
                for c in range(CT):
                    last = pe.matmul(ps[:, 1, c:c + 1], membt[:, c, :], gstat[:, 0:1], start=True, stop=True)
                last.then_inc(norm_pe, 1)
                pe.wait_ge(norm_dve, 7 * lb + 5)
                for c in range(CT):
                    last = pe.matmul(ps[0:GROUPS, 2, 0:1], memb[:, c, :], cvar[:, c:c + 1], start=(c == 0), stop=(c == CT - 1))
                last.then_inc(norm_pe, 1)
                pe.wait_ge(norm_pool, lb + 1)
                for c in range(CT):
                    last = pe.matmul(ps[:, 3, c:c + 1], membt[:, c, :], gstat[:, 2:3], start=True, stop=True)
                last.then_inc(norm_pe, 1)

                pe.wait_ge(xs_ready, CT * (lb + 1))

                def qk_tile(m):
                    if m % 2 == 0:
                        pe.wait_ge(ws_ready, CHUNKS * lb + m // 2 + 3)
                    last = transposed_weights_tile(m // 2 % 2, m % 2, D(m % 4))
                    last.then_inc(mt_done, 1)

                for m in range(CT):
                    if m >= 4:
                        pe.wait_ge(mt_act, CT * lb + m - 3)
                        pe.wait_ge(mt_dve, 3 * CT * lb + 2 * (m - 3))
                    qk_tile(m)
                pe.wait_ge(mt_act, CT * (lb + 1))
                pe.wait_ge(mt_dve, 3 * CT * lb + 2 * CT)
                pe.wait_ge(tab_ready, 6 * (lb + 1))
                grid = qT.rearrange("p m (h w) -> p m h w", h=HW)
                for r in range(HW):
                    if r >= 8:
                        pe.wait_ge(rel_act, HW * lb + r - 7)
                        pe.wait_ge(rel_dve, HW * lb + r - 7)
                    for i in range(2):
                        at = 2 * (r % (HW // 2)) + i
                        back = HW - 1 - at
                        if r < HW // 2:
                            moving, table = grid[:, :, at, :], by_row[:, back, :]
                        else:
                            moving, table = grid[:, :, :, at], by_col[back // 24][:, back % 24, :]
                        M = table.shape[-1]
                        last = pe.matmul(ps[0:M, r % 8, i * CT * HW:(i + 1) * CT * HW].rearrange("p (m w) -> p m w", m=CT),
                                         table, moving, start=True, stop=True)
                    last.then_inc(rel_done, 1)
                pe.wait_ge(rel_act, HW * (lb + 1))
                pe.wait_ge(rel_dve, HW * (lb + 1))
                for m in range(CT, 2 * CT):
                    if m >= CT + 4:
                        pe.wait_ge(mt_dve, 3 * CT * lb + 2 * CT + m - CT - 3)
                    qk_tile(m)
                pe.wait_ge(mt_dve, 3 * CT * (lb + 1))
                for j in range(2 * CT // 2, QKV_CHUNKS):
                    pe.wait_ge(ws_ready, CHUNKS * lb + j + 3)
                    for t in range(TT):
                        d = 2 * (j - CT) + t // 4
                        if d >= 4 and t % 4 == 0:
                            pe.wait_ge(v_evac, CT * lb + d - 3)
                        last = token_tile(j % 2, t, D(d % 4)[:, t % 4 * WC:(t % 4 + 1) * WC])
                        if t % 4 == 3:
                            last.then_inc(v_done, 1)
                pe.wait_ge(v_evac, CT * (lb + 1))
                n0 = HEADS * lb
                for j in range(TT):
                    max_tile(0, n0, j, guarded=False)
                max_row(0, n0)
                pe.wait_ge(fill_dve, 8 * (lb + 1))
                for u in range(AHEAD):
                    scores(0, n0, u, None, guarded=False)
                for u in (6, 7):
                    for j in MAX_AT[u]:
                        max_tile(1, n0 + 1, j)
                with pe.Fori(0, PAIRS - 1) as p:
                    pair(PAIRS * lb + p, False)
                pair(PAIRS * lb + PAIRS - 1, True)
                pe.wait_ge(as_ready, CT * (lb + 1))
                pe.wait_ge(out_taken, 2 * HEADS * (lb + 1) + 2)
                pe.wait_ge(sum_taken, 2 * HEADS * (lb + 1) + 2)
                for j in range(QKV_CHUNKS, CHUNKS):
                    pe.wait_ge(ws_ready, CHUNKS * lb + j + 3)
                    for t in range(TT):
                        d = 2 * (j - QKV_CHUNKS) + t // 4
                        if d >= 4 and t % 4 == 0:
                            pe.wait_ge(y_evac, CT * lb + d - 3 + 1)
                        last = token_tile(j % 2, t, D(d % 4)[:, t % 4 * WC:(t % 4 + 1) * WC])
                        if t % 4 == 3:
                            last.then_inc(y_done, 1)

        @block.scalar
        def _(act):
            def copy(out, in_):
                return act.activation(out, in_, ACT.Copy)

            def w_high(lb, j):
                act.wait_ge(w_loaded[j % 2], 16 * (CHUNKS // 2 * lb + j // 2 + 1))
                copy(wsplit(j % 2, 0), wraw[:, j % 2, :, :]).then_inc(wh_ready, 1)

            def split_qk(e, pr):
                copy(Kh[e][own[e], :], k32[own[e], bass.ds(pr, 1), :].rearrange("p a s -> p (a s)")).then_inc(kh_ready, 1)
                copy(Q3[e][own[e], :], qa[e][own[e], bass.ds(pr, 1), :].rearrange("p a s -> p (a s)")).then_inc(q3_ready, 1)

            def split_v(e, pr):
                copy(V1[e][:, :, own[e]], v32[:, :, bass.ds(pr * P + e * HD, HD)]).then_inc(v1_ready, 1)

            def row(e, n):
                act.wait_ge(row_done, n + 1)
                r = first_other[e]
                copy(Q3[e][r:r + 1, :], D(2)[0:1, :]).then_inc(row_ready, 1)

            def exps(u, s):
                act.wait_ge(sc_done, s + 1)
                act.wait_ge(lo_ready, s + 1)
                act.activation(p32[:, u % 2, :], D(u % 2), ACT.Exp).then_inc(probs_ready, 1)
                act.wait_ge(pv_done, s + 1)
                act.activation(Ph[u % 2], D(u % 2), ACT.Exp).then_inc(probs_ready, 1)

            def out_half(e, pr, s, half):
                act.wait_ge(pv_done, s + 3)
                copy(attn[own[e], bass.ds(pr, 1), half * HALF:(half + 1) * HALF].rearrange("p a s -> p (a s)"),
                     ps[own[e], 6 + half, :]).then_inc(out_taken, 1)

            def pair(lb, p, last_pair):
                g = PAIRS * lb + p
                for t in range(2 * STEPS):
                    e, u = t // STEPS, t % STEPS
                    n, s = 2 * g + e, 2 * STEPS * g + t
                    if u == ROW_AT and not (last_pair and e == 1):
                        row(1 - e, n + 1)
                    if not (last_pair and t + AHEAD >= 2 * STEPS):
                        exps((t + AHEAD) % STEPS, s + AHEAD)
                    if u % 4 == 3:
                        out_half(e, p, s, u // 4)
                    if u == 1 and not (last_pair and e == 1):
                        act.wait_ge(pv_done, STEPS * n + 2)
                        split_v(1 - e, p + e)
                    if u == ROW_AT and not last_pair:
                        act.wait_ge(sc_done, STEPS * (n + 1))
                        split_qk(e, p + 1)

            with act.Fori(0, LAYERS * B) as lb:
                for c in range(CT):
                    act.wait_ge(tr_done, CT * lb + c + 1)
                    copy(xT[:, c, :], D(c % 4)).then_inc(xt_ready, 1)
                for j in range(2):
                    w_high(lb, j)
                for c in range(CT):
                    act.wait_ge(xn_ready, CT * lb + c + 1)
                    copy(xh[:, c, :], xT[:, c, :]).then_inc(xh_ready, 1)
                act.wait_ge(small, 32 * (lb + 1))
                act.wait_ge(tab_zero, 2 * (lb + 1))
                for e, at_row, at_col in ((0, 64, 96), (1, 0, 32)):
                    for dst, at, first in ((by_row, at_row, 0), (by_col[0], at_col, 0), (by_col[1], at_col, 24)):
                        kind, count = int(dst is not by_row), dst.shape[1]
                        copy(dst[own[e], :, at:at + HW], windows(e, kind, first, count)).then_inc(tab_ready, 1)
                for m in range(CT):
                    act.wait_ge(mt_done, 2 * CT * lb + m + 1)
                    act.activation(qT[:, m, :], D(m % 4), ACT.Identity, bias=qkb[:, m:m + 1]).then_inc(mt_act, 1)
                    if m % 2:
                        w_high(lb, m // 2 + 2)
                for r in range(HW):
                    act.wait_ge(rel_done, HW * lb + r + 1)
                    rel_out(act.activation, ps, qa[1], r, 0, True).then_inc(rel_act, 1)
                for m in range(CT + 1, 2 * CT, 2):
                    act.wait_ge(mt_done, 2 * CT * lb + m + 1)
                    w_high(lb, m // 2 + 2)
                act.wait_ge(v_done, CT * lb + 2)
                w_high(lb, QKV_CHUNKS - 1)
                act.wait_ge(v_done, CT * (lb + 1))
                for e in range(2):
                    copy(Kh[e][other[e], :], hot[other[e], :])
                    split_qk(e, 0)
                    if e == 0:
                        act.wait_ge(v_evac, CT * (lb + 1))
                        split_v(0, 0)
                        act.wait_ge(fill_dve, 8 * (lb + 1))
                        row(0, HEADS * lb)
                for u in range(AHEAD):
                    exps(u, 2 * STEPS * PAIRS * lb + u)
                with act.Fori(0, PAIRS - 1) as p:
                    pair(lb, p, False)
                pair(lb, PAIRS - 1, True)
                w_high(lb, QKV_CHUNKS)
                w_high(lb, QKV_CHUNKS + 1)
                for c in range(CT):
                    act.wait_ge(an_ready, CT * lb + c + 1)
                    copy(xh[:, c, :], attn[:, c, :]).then_inc(ah_ready, 1)
                act.wait_ge(y_done, CT * lb + 2)
                w_high(lb, QKV_CHUNKS + 2)

        @block.vector
        def _(dve):
            for ring, free in ((ws_ready, 2), (lo_ready, 2), (pv_done, 2), (out_taken, 2), (sum_taken, 2),
                               (y_evac, 1), (sum_stored[0], 16), (sum_stored[1], 16)):
                dve.sem_inc(ring, free)

            def max_take(e, n, j):
                dve.wait_ge(max_done, STEPS * n + j + 1)
                dve.tensor_reduce(nmax[:, e, j:j + 1], D(2), AX_X, ALU.max, negate=True).then_inc(max_taken, 1)

            def low(u, s):
                dve.wait_ge(probs_ready, 2 * (s + 1))
                dve.wait_ge(pv_done, s + 1)
                dve.tensor_tensor(Pl[u % 2], p32[:, u % 2, :], Ph[u % 2], ALU.subtract).then_inc(lo_ready, 1)

            def query_high(e, pr):
                dve.tensor_copy(Qh[e], qa[e][:, bass.ds(pr, 1), :].rearrange("p a s -> p (a s)")).then_inc(qh_ready, 1)

            def sum_half(e, g, s, half):
                dve.wait_ge(pv_done, s + 3)
                if half == 0:
                    dve.wait_ge(sum_stored[e], 16 * g + 16)
                r = first_other[e]
                dve.tensor_copy(sumrow[r:r + 1, half * HALF:(half + 1) * HALF], ps[r:r + 1, 6 + half, :]).then_inc(sum_taken, 1)

            def pair(lb, p, last_pair):
                g = PAIRS * lb + p
                for t in range(2 * STEPS):
                    e, u = t // STEPS, t % STEPS
                    n, s = 2 * g + e, 2 * STEPS * g + t
                    ahead = 2 if u > ROW_AT else 1
                    tiles = [] if last_pair and e + ahead > 1 else MAX_AT.get(u, [])
                    for j in tiles:
                        max_take((e + ahead) % 2, n + ahead, j)
                    if not (last_pair and t + AHEAD >= 2 * STEPS):
                        low((t + AHEAD) % STEPS, s + AHEAD)
                    if u % 4 == 3:
                        sum_half(e, g, s, u // 4)
                    if u == ROW_AT and not last_pair:
                        dve.wait_ge(sc_done, STEPS * (n + 1))
                        query_high(e, p + 1)

            with dve.Fori(0, LAYERS * B) as lb:
                nd = 7 * lb
                for c in range(CT):
                    dve.wait_ge(xt_ready, CT * lb + c + 1)
                    for half in range(2):
                        dve.bn_stats(stats[:, c, 6 * half:6 * half + 6], xT[:, c, half * HALF:(half + 1) * HALF]).then_inc(stat_ready, 1)
                dve.wait_ge(stat_ready, 2 * CT * (lb + 1))
                dve.sem_inc(gate, 1)
                for c in range(CT):
                    dve.bn_aggr(mv[:, c, :], stats[:, c, :]).then_inc(aggr_ready, 1)
                dve.wait_ge(norm_pe, 4 * lb + 1)
                dve.tensor_copy(gstat[:, 0:1], ps[0:GROUPS, 0, 0:1]).then_inc(norm_dve, 1)
                dve.wait_ge(norm_pe, 4 * lb + 2)
                dve.tensor_copy(cmean[:, :], ps[:, 1, 0:CT]).then_inc(norm_dve, 1)
                dve.wait_ge(norm_dve, nd + 2)
                dve.tensor_tensor(dev[:, :], mv[:, :, 0], cmean[:, :], ALU.subtract).then_inc(norm_dve, 1)
                dve.wait_ge(norm_dve, nd + 3)
                dve.tensor_tensor(dev2[:, :], dev[:, :], dev[:, :], ALU.mult).then_inc(norm_dve, 1)
                dve.wait_ge(norm_dve, nd + 4)
                dve.tensor_tensor(cvar[:, :], dev2[:, :], mv[:, :, 1], ALU.add).then_inc(norm_dve, 1)
                dve.wait_ge(norm_pe, 4 * lb + 3)
                dve.tensor_scalar(gstat[:, 1:2], ps[0:GROUPS, 2, 0:1], EPS, None, ALU.add).then_inc(norm_dve, 1)
                dve.wait_ge(norm_pe, 4 * lb + 4)
                dve.tensor_copy(crstd[:, :], ps[:, 3, 0:CT]).then_inc(norm_dve, 1)
                dve.wait_ge(norm_dve, nd + 7)
                for c in range(CT):
                    dve.tensor_scalar(xT[:, c, :], xT[:, c, :], cmean[:, c:c + 1], crstd[:, c:c + 1],
                                      ALU.subtract, ALU.mult).then_inc(xn_ready, 1)
                for c in range(CT):
                    dve.wait_ge(xh_ready, CT * lb + c + 1)
                    dve.tensor_tensor(xl[:, c, :], xT[:, c, :], xh[:, c, :], ALU.subtract).then_inc(xs_ready, 1)
                dve.wait_ge(small, 32 * (lb + 1))
                for m in range(CT):
                    dve.wait_ge(mt_act, CT * lb + m + 1)
                    if m == 0:
                        dve.wait_ge(xs_ready, CT * (lb + 1))
                    for e in range(2):
                        dve.tensor_scalar(qa[e][own[e], m, :], D(m % 4)[own[e], :], qkb[own[e], m:m + 1], None,
                                          ALU.add).then_inc(mt_dve, 1)
                for r in range(HW):
                    dve.wait_ge(rel_done, HW * lb + r + 1)
                    rel_out(dve.tensor_copy, ps, qa[0], r, HD, False).then_inc(rel_dve, 1)
                for m in range(CT):
                    dve.wait_ge(mt_done, 2 * CT * lb + CT + m + 1)
                    dve.tensor_scalar(k32[:, m, :], D((CT + m) % 4), qkb[:, CT + m:CT + m + 1], SCALE,
                                      ALU.add, ALU.mult).then_inc(mt_dve, 1)
                dve.wait_ge(rowb_loaded, 32 * lb + 16)
                for d in range(CT):
                    dve.wait_ge(v_done, CT * lb + d + 1)
                    t0, cols = d % 2 * 4, slice(d // 2 * WC, (d // 2 + 1) * WC)
                    bias = rowb[:, cols].rearrange("p (a n) -> p a n", a=1).to_broadcast([P, 4, WC])
                    dve.tensor_tensor(v32[:, t0:t0 + 4, cols], D(d % 4).rearrange("p (t n) -> p t n", t=4), bias,
                                      ALU.add).then_inc(v_evac, 1)
                query_high(0, 0)
                for e in range(2):
                    dve.memset(Q3[e][other[e], :].bitcast(F32), 0.0).then_inc(fill_dve, 1)
                    dve.memset(K3[e][other[e], :].bitcast(F32), 1.0).then_inc(fill_dve, 1)
                    dve.memset(V1[e][:, :, other[e]].bitcast(F32), 1.0).then_inc(fill_dve, 1)
                    dve.memset(V0[e][:, :, other[e]].bitcast(F32), 0.0).then_inc(fill_dve, 1)
                query_high(1, 0)
                for j in range(TT):
                    max_take(0, HEADS * lb, j)
                for u in range(AHEAD):
                    low(u, 2 * STEPS * PAIRS * lb + u)
                for u in (6, 7):
                    for j in MAX_AT[u]:
                        max_take(1, HEADS * lb + 1, j)
                with dve.Fori(0, PAIRS - 1) as p:
                    pair(lb, p, False)
                pair(lb, PAIRS - 1, True)
                dve.wait_ge(rs_loaded, 16 * (lb + 1))
                dve.reciprocal(rs[:, :], rs[:, :]).then_inc(rs_ready, 1)
                dve.wait_ge(recip_loaded, 32 * (lb + 1))
                dve.wait_ge(out_taken, 2 * HEADS * (lb + 1) + 2)
                for c in range(CT):
                    dve.tensor_tensor(attn[:, c, :], attn[:, c, :], recip[:, c, :], ALU.mult).then_inc(an_ready, 1)
                for c in range(CT):
                    dve.wait_ge(ah_ready, CT * lb + c + 1)
                    dve.tensor_tensor(xl[:, c, :], attn[:, c, :], xh[:, c, :], ALU.subtract).then_inc(as_ready, 1)
                dve.wait_ge(xb_ready, TT * (lb + 1))
                for d in range(CT):
                    dve.wait_ge(y_done, CT * lb + d + 1)
                    t0, cols = d % 2 * 4, slice(d // 2 * WC, (d // 2 + 1) * WC)
                    out = xin[:, t0:t0 + 4, cols]
                    dve.tensor_tensor(out, D(d % 4).rearrange("p (t n) -> p t n", t=4), out, ALU.add).then_inc(y_evac, 1)

        @block.gpsimd
        def _(pool):
            pool.memset(gstat[:, 3:4], -0.5).then_inc(primed, 1)
            pool.wait_ge(primed, 1)

            def w_low(lb, j):
                pool.wait_ge(wh_ready, CHUNKS * lb + j + 1)
                pool.tensor_tensor(wsplit(j % 2, 1), wraw[:, j % 2, :, :], wsplit(j % 2, 0), ALU.subtract).then_inc(ws_ready, 1)

            def split_qk(e, pr, n):
                pool.wait_ge(qh_ready, n + 1)
                pool.tensor_tensor(Ql[e], qa[e][:, bass.ds(pr, 1), :].rearrange("p a s -> p (a s)"), Qh[e],
                                   ALU.subtract).then_inc(low_ready, 1)
                pool.wait_ge(kh_ready, n + 1)
                pool.wait_ge(low_ready, 2 * n + 1)
                pool.tensor_tensor(K3[e][own[e], :], k32[own[e], bass.ds(pr, 1), :].rearrange("p a s -> p (a s)"),
                                   Kh[e][own[e], :], ALU.subtract).then_inc(low_ready, 1)
                pool.wait_ge(low_ready, 2 * (n + 1))
                pool.sem_inc(gate, 1)

            def split_v(e, pr, n):
                pool.wait_ge(v1_ready, n + 1)
                pool.tensor_tensor(V0[e][:, :, own[e]], v32[:, :, bass.ds(pr * P + e * HD, HD)], V1[e][:, :, own[e]],
                                   ALU.subtract).then_inc(v0_ready, 1)

            with pool.Fori(0, LAYERS * B) as lb:
                pool.wait_ge(x_loaded, 16 * (lb + 1))
                pool.sem_inc(gate, 1)
                pool.memset(k32_flat, 0.0).then_inc(tab_zero, 1)
                pool.memset(sumrow[:, :], 0.0).then_inc(tab_zero, 1)
                w_low(lb, 0)
                w_low(lb, 1)
                pool.wait_ge(norm_dve, 7 * lb + 6)
                pool.tensor_tensor(gstat[:, 2:3], gstat[:, 1:2], gstat[:, 3:4], ALU.pow).then_inc(norm_pool, 1)
                for j in range(2, QKV_CHUNKS):
                    w_low(lb, j)
                n0 = HEADS * lb
                split_qk(0, 0, n0)
                split_v(0, 0, n0)
                split_qk(1, 0, n0 + 1)
                with pool.Fori(0, PAIRS - 1) as p:
                    for e in range(2):
                        n = n0 + 2 * p + e
                        split_v(1 - e, p + e, n + 1)
                        split_qk(e, p + 1, n + 2)
                split_v(1, PAIRS - 1, n0 + HEADS - 1)
                w_low(lb, QKV_CHUNKS)
                w_low(lb, QKV_CHUNKS + 1)
                pool.wait_ge(resid_loaded, 16 * (lb + 1))
                pool.wait_ge(rowb_loaded, 32 * (lb + 1))
                for t in range(TT):
                    pool.tensor_tensor(xin[:, t, :], xin[:, t, :], rowb[:, :], ALU.add).then_inc(xb_ready, 1)
                w_low(lb, QKV_CHUNKS + 2)


def kernel(x, L0_conv_Wqkv, L0_conv_Wproj, L0_conv_bproj, L0_conv_rel_pos_h, L0_conv_rel_pos_w,
           L1_conv_qkv_w, L1_conv_qkv_b, L1_conv_proj_w, L1_conv_proj_b, L1_conv_rel_pos_h, L1_conv_rel_pos_w):
    import numpy as np
    import concourse.bacc as bacc
    from concourse.bass_utils import run_bass_kernel_spmd

    def f(a):
        return np.asarray(a)

    rel = np.zeros((LAYERS, P, 2, OFFS), np.float32)
    for l, (rh, rw) in enumerate(((L0_conv_rel_pos_h, L0_conv_rel_pos_w), (L1_conv_rel_pos_h, L1_conv_rel_pos_w))):
        for i, table in enumerate((rh, rw)):
            t = f(table)[:OFFS][::-1].T
            rel[l, :HD, i] = rel[l, HD:, i] = t
    qkv_b = np.stack([np.zeros(3 * C, np.float32), f(L1_conv_qkv_b)])
    tok = np.arange(S)
    codes = np.concatenate([np.arange(HW)[:, None] == tok // HW, np.arange(HW)[:, None] == tok % HW]).astype(np.float32)
    group = np.arange(C) // (C // GROUPS)
    member = (group[:, None] == np.arange(GROUPS)).astype(np.float32)
    arrays = {
        "x": f(x).reshape(B, S, C),
        "wqkv": np.stack([f(L0_conv_Wqkv), f(L1_conv_qkv_w)]),
        "wproj": np.stack([f(L0_conv_Wproj), f(L1_conv_proj_w)]),
        "qk_bias": np.ascontiguousarray(qkv_b[:, :2 * C].reshape(LAYERS, 2 * CT, P).transpose(0, 2, 1)),
        "v_bias": np.ascontiguousarray(qkv_b[:, 2 * C:]),
        "proj_bias": np.stack([f(L0_conv_bproj), f(L1_conv_proj_b)]),
        "rel": rel,
        "onehot": np.concatenate([codes, codes]),
        "ident": np.eye(P, dtype=np.float32),
        "member": np.ascontiguousarray(member.reshape(CT, P, GROUPS).transpose(1, 0, 2)) / np.float32(C // GROUPS),
        "member_t": np.ascontiguousarray(member.T.reshape(GROUPS, CT, P)),
    }
    nc = bacc.Bacc("TRN2", target_bir_lowering=False, num_devices=1)
    ins = [nc.dram_tensor(f"in_{k}", a.shape, mybir.dt.from_np(a.dtype), kind="ExternalInput").ap() for k, a in arrays.items()]
    out = nc.dram_tensor("state", ((LAYERS + 1) * B, S, C), F32, kind="ExternalOutput").ap()
    two_layers(nc, *ins, out)
    r = run_bass_kernel_spmd(nc, [{f"in_{k}": a for k, a in arrays.items()}], core_ids=[0])
    return r.results[0]["state"][LAYERS * B:].reshape(B, HW, HW, C)
```

```python
from contextlib import ExitStack

import concourse.bass as bass
from concourse import mybir

F32 = mybir.dt.float32
F32R = mybir.dt.float32r
ALU = mybir.AluOpType
ACT = mybir.ActivationFunctionType
AX_X = mybir.AxisListType.X

P = 128
LAYERS, B, HW, C = 2, 4, 32, 768
S = HW * HW
HEADS, HD = 12, 64
PAIRS = HEADS // 2
CT = C // P
TT = S // P
GROUPS = 32
HALF = 512
WC = 256
QKV_CHUNKS, PROJ_CHUNKS = 3 * C // WC, C // WC
CHUNKS = QKV_CHUNKS + PROJ_CHUNKS
OFFS = 2 * HW - 1
SCALE = HD ** -0.5
EPS = 1e-5
STEPS = 8
AHEAD = 2
MAX_AT = {6: [0], 7: [1], 0: [2], 1: [3], 2: [4], 3: [5, 6], 4: [7]}
EARLY = HEADS - 2
ROW_AT = 5
MAX_FIRST = (3, 4)


def two_layers(nc, x, wqkv, wproj, qk_bias, v_bias, proj_bias, rel, code, ident, member, member_t,
               state):
    with ExitStack() as ctx:
        def sb(name, shape, dt=F32):
            return ctx.enter_context(nc.sbuf_tensor(name, shape, dt))

        def sem(name):
            return ctx.enter_context(nc.semaphore(name))

        sums_dram = nc.dram_tensor("sums_scratch", (LAYERS * B, HEADS, S), F32, kind="Internal").ap()
        recips_dram = nc.dram_tensor("recips_scratch", (LAYERS * B, HEADS, S), F32, kind="Internal").ap()

        qa = [sb("q_even", [P, CT, S]), sb("q_odd", [P, CT, S])]
        xT = qa[0]
        attn = qa[0]
        k32 = sb("k32", [P, CT, S])
        recip = k32
        v32 = sb("v32", [P, TT, C])
        resid = v32
        qT = v32[:, :, :].rearrange("p t c -> p (t c)").rearrange("p (m s) -> p m s", m=CT)
        wraw = sb("wraw", [P, 2, CT, WC])
        p32 = sb("p32", [P, 2, S])
        xin = qa[1][:, :, :].rearrange("p m s -> p (m s)").rearrange("p (t c) -> p t c", t=TT)
        sumrow = sb("sumrow", [P, S])
        codes = sb("codes", [P, S])
        idt = sb("idt", [P, P])
        tab = sb("tab", [P, 2, OFFS])
        qkb = sb("qkb", [P, 2 * CT])
        rowb = sb("rowb", [P, C])
        memb = sb("memb", [P, CT, GROUPS])
        membt = sb("membt", [GROUPS, CT, P])
        stats = sb("stats", [P, CT, 12])
        mv = sb("mv", [P, CT, 2])
        gstat = sb("gstat", [GROUPS, 4])
        cmean = sb("cmean", [P, CT])
        crstd = sb("crstd", [P, CT])
        dev = sb("dev", [P, CT])
        dev2 = sb("dev2", [P, CT])
        cvar = sb("cvar", [P, CT])
        nmax = sb("nmax", [P, 2, TT])
        rs = sb("rs", [P, EARLY * S // P])

        k32_flat = k32[:, :, :].rearrange("p m s -> p (m s)")
        by_row = k32_flat[:, 0:HW * 96].rearrange("p (a n) -> p a n", n=96)
        by_col = [k32_flat[:, HW * 96:].rearrange("p (a n) -> p a n", n=P),
                  sumrow[:, :].rearrange("p (a n) -> p a n", n=P)]

        def windows(e, kind, first, count):
            base = tab[own[e], kind, first:first + 1]
            return bass.AP(tensor=base.tensor, offset=base.offset, ap=[list(base.ap[0]), [1, count], [1, HW]])

        R = sb("R", [P, 18 * S], F32R)

        def rtile(i):
            return R[:, i * S:(i + 1) * S]

        Qh, Kh, Ql, Q3, K3 = ([rtile(7 * e + i) for e in range(2)] for i in range(5))
        V1, V0 = ([rtile(7 * e + i).rearrange("p (t m) -> p t m", t=TT) for e in range(2)] for i in (5, 6))
        Ph = [rtile(14), rtile(15)]
        Pl = [rtile(16), rtile(17)]
        xh = [rtile(3 + 2 * k) for k in range(CT)]
        xl = [rtile(4 + 2 * k) for k in range(CT)]

        def wsplit(slot, low):
            o = (0 if slot else 15 * S) + low * CT * WC
            return R[:, o:o + CT * WC].rearrange("p (k n) -> p k n", k=CT)

        own = [slice(0, HD), slice(HD, P)]
        other = [slice(HD, P), slice(0, HD)]
        first_other = [HD, 0]

        ps = ctx.enter_context(nc.psum_tensor("ps", [P, 8, HALF], F32))

        def D(i):
            return ps[:, 2 * i:2 * i + 2, :].rearrange("p a n -> p (a n)")

        consts = sem("consts")
        small = sem("small")
        rowb_loaded = sem("rowb_loaded")
        x_loaded = sem("x_loaded")
        resid_loaded = sem("resid_loaded")
        copied = sem("copied")
        w_loaded = [sem("w_loaded0"), sem("w_loaded1")]
        primed = sem("primed")
        gate = sem("gate")
        tab_zero = sem("tab_zero")
        tab_ready = sem("tab_ready")
        tr_done = sem("tr_done")
        xt_ready = sem("xt_ready")
        stat_ready = sem("stat_ready")
        aggr_ready = sem("aggr_ready")
        norm_pe = sem("norm_pe")
        norm_dve = sem("norm_dve")
        norm_pool = sem("norm_pool")
        xn_ready = sem("xn_ready")
        xh_ready = sem("xh_ready")
        xs_ready = sem("xs_ready")
        wh_ready = sem("wh_ready")
        ws_ready = sem("ws_ready")
        mt_done = sem("mt_done")
        mt_act = sem("mt_act")
        mt_dve = sem("mt_dve")
        rel_done = sem("rel_done")
        rel_act = sem("rel_act")
        rel_dve = sem("rel_dve")
        v_done = sem("v_done")
        v_evac = sem("v_evac")
        fill_dve = sem("fill_dve")
        qh_ready = sem("qh_ready")
        kh_ready = sem("kh_ready")
        q3_ready = sem("q3_ready")
        low_ready = sem("low_ready")
        v1_ready = sem("v1_ready")
        v0_ready = sem("v0_ready")
        max_done = sem("max_done")
        max_taken = sem("max_taken")
        row_done = sem("row_done")
        row_ready = sem("row_ready")
        sc_done = sem("sc_done")
        probs_ready = sem("probs_ready")
        lo_ready = sem("lo_ready")
        pv_done = sem("pv_done")
        out_taken = sem("out_taken")
        sum_taken = sem("sum_taken")
        sum_stored = [sem("sum_stored0"), sem("sum_stored1")]
        rs_loaded = sem("rs_loaded")
        rs_ready = sem("rs_ready")
        rs_stored = sem("rs_stored")
        recip_loaded = sem("recip_loaded")
        an_ready = sem("an_ready")
        ah_ready = sem("ah_ready")
        as_ready = sem("as_ready")
        xb_ready = sem("xb_ready")
        y_done = sem("y_done")
        y_evac = sem("y_evac")
        stored = sem("stored")

        block = ctx.enter_context(nc.Block())

        def rel_out(op, ps, dst, r, base, on_act):
            at = 2 * (r % (HW // 2))
            by_row = r < HW // 2
            q = base + (0 if by_row else HW)
            grid = dst[q:q + HW, :, :].rearrange("p m (h w) -> p m h w", h=HW)
            if by_row:
                out = grid[:, :, at:at + 2, :].rearrange("p m a w -> p a m w")
            else:
                out = grid[:, :, :, at:at + 2].rearrange("p m h a -> p a m h")
            in_ = ps[q:q + HW, r % 8, 0:2 * CT * HW].rearrange("p (a m w) -> p a m w", a=2, m=CT)
            return op(out, in_, ACT.Copy) if on_act else op(out, in_)

        @block.sync
        def _(sp):
            for dst, src in ((idt, ident), (codes, code), (memb, member), (membt, member_t)):
                sp.dma_start(dst[tuple([slice(None)] * len(dst.shape))], src).then_inc(consts, 16)
            sp.dma_start(xin, x[0].rearrange("(t p) c -> p t c", p=P)).then_inc(x_loaded, 16)

            def load_chunk(n, layer, j):
                sp.wait_ge(ws_ready, CHUNKS * n + j + 1)
                sp.sem_inc(gate, 1)
                w, c0 = (wqkv, j * WC) if j < QKV_CHUNKS else (wproj, (j - QKV_CHUNKS) * WC)
                src = w[bass.ds(layer, 1), :, c0:c0 + WC].rearrange("a (k p) n -> p (a k) n", p=P)
                sp.dma_start(wraw[:, j % 2, :, :], src).then_inc(w_loaded[j % 2], 16)

            load_chunk(0, 0, 0)
            load_chunk(0, 0, 1)
            sp.dma_start(state[0:B], x).then_inc(copied, 16)

            with sp.Fori(0, LAYERS * B) as lb:
                layer = lb // B
                sp.dma_start(tab[:, :, :], rel[bass.ds(layer, 1)].rearrange("a p r n -> p (a r) n")).then_inc(small, 16)
                sp.dma_start(qkb[:, :], qk_bias[bass.ds(layer, 1)].rearrange("a p m -> p (a m)")).then_inc(small, 16)
                sp.dma_start(rowb[:, :], v_bias[bass.ds(layer, 1)].to_broadcast([P, C])).then_inc(rowb_loaded, 16)
                for j in range(2, QKV_CHUNKS):
                    load_chunk(lb, layer, j)
                sp.wait_ge(v_evac, CT * (lb + 1))
                sp.sem_inc(gate, 1)
                sp.dma_start(rowb[:, :], proj_bias[bass.ds(layer, 1)].to_broadcast([P, C])).then_inc(rowb_loaded, 16)
                load_chunk(lb, layer, QKV_CHUNKS)
                load_chunk(lb, layer, QKV_CHUNKS + 1)

                with sp.Fori(0, PAIRS - 1) as p:
                    for e in range(2):
                        sp.wait_ge(sum_taken, 2 * (2 * (PAIRS * lb + p) + e) + 4)
                        sp.sem_inc(gate, 1)
                        r = first_other[e]
                        sp.dma_start(sums_dram[bass.ds(lb, 1), bass.ds(2 * p + e, 1), :].rearrange("a h s -> (a h) s"),
                                     sumrow[r:r + 1, :]).then_inc(sum_stored[e], 16)
                for e in range(2):
                    sp.wait_ge(sum_stored[e], 16 * (PAIRS - 1) * (lb + 1) + 16)
                    sp.sem_inc(gate, 1)
                sp.dma_start(rs[:, :], sums_dram[bass.ds(lb, 1), 0:EARLY].rearrange("a h s -> (a h s)").rearrange("(p n) -> p n", p=P)).then_inc(rs_loaded, 16)
                sp.wait_ge(v0_ready, HEADS * (lb + 1))
                sp.sem_inc(gate, 1)
                sp.wait_ge(copied, 16)
                sp.sem_inc(gate, 1)
                sp.dma_start(resid[:, :, :], state[bass.ds(lb, 1)].rearrange("a (t p) c -> p (a t) c", p=P)).then_inc(resid_loaded, 16)
                sp.wait_ge(rs_ready, lb + 1)
                sp.sem_inc(gate, 1)
                sp.dma_start(recips_dram[bass.ds(lb, 1), 0:EARLY].rearrange("a h s -> (a h s)").rearrange("(p n) -> p n", p=P), rs[:, :]).then_inc(rs_stored, 16)
                sp.wait_ge(rs_stored, 16 * (lb + 1))
                sp.sem_inc(gate, 1)
                sp.wait_ge(low_ready, 2 * HEADS * (lb + 1))
                sp.sem_inc(gate, 1)
                for e in range(2):
                    src = recips_dram[bass.ds(lb, 1), 0:EARLY].rearrange("a (p e) s -> a e p s", e=2)[:, e].to_broadcast([HD, PAIRS - 1, S])
                    sp.dma_start(recip[own[e], 0:PAIRS - 1, :], src).then_inc(recip_loaded, 16)
                sp.wait_ge(q3_ready, HEADS * (lb + 1))
                sp.sem_inc(gate, 1)
                sp.dma_start(xin, state[bass.ds(lb + 1, 1)].rearrange("a (t p) c -> p (a t) c", p=P)).then_inc(x_loaded, 16)
                load_chunk(lb, layer, QKV_CHUNKS + 2)
                following = (lb + 1) % (LAYERS * B) // B
                load_chunk(lb + 1, following, 0)
                load_chunk(lb + 1, following, 1)
                sp.wait_ge(y_evac, CT * (lb + 1) + 1)
                sp.sem_inc(gate, 1)
                sp.dma_start(state[bass.ds(lb + B, 1)].rearrange("a (t p) c -> p (a t) c", p=P), resid[:, :, :]).then_inc(stored, 16)
            sp.wait_ge(stored, 16 * LAYERS * B + 16)
            sp.sem_inc(gate, 1)

        @block.tensor
        def _(pe):
            def three(out, a, b, first, last):
                pe.matmul(out, a[0], b[0], start=first, stop=False)
                pe.matmul(out, a[0], b[1], start=False, stop=False)
                return pe.matmul(out, a[1], b[0], start=False, stop=last)

            def transposed_weights_tile(slot, m, dst, first_image_tile=None):
                cols = slice(m * P, (m + 1) * P)
                for half in range(2):
                    toks = slice(half * HALF, (half + 1) * HALF)
                    for k in range(CT):
                        if first_image_tile is not None and half == 0:
                            pe.wait_ge(xs_ready, CT * first_image_tile + k + 1)
                        last = three(dst[:, toks], (wsplit(slot, 0)[:, k, cols], wsplit(slot, 1)[:, k, cols]),
                                     (xh[k][:, toks], xl[k][:, toks]), k == 0, k == CT - 1)
                return last

            def token_tile(slot, t, dst):
                toks = slice(t * P, (t + 1) * P)
                for k in range(CT):
                    last = three(dst, (xh[k][:, toks], xl[k][:, toks]),
                                 (wsplit(slot, 0)[:, k, :], wsplit(slot, 1)[:, k, :]), k == 0, k == CT - 1)
                return last

            def max_tile(e, n, j, guarded=True):
                if j == 0:
                    pe.wait_ge(qh_ready, n + 1)
                    pe.wait_ge(kh_ready, n + 1)
                    if guarded:
                        pe.wait_ge(row_ready, n)
                else:
                    pe.wait_ge(max_taken, STEPS * n + j)
                for half in range(2):
                    ks = slice(half * HALF, (half + 1) * HALF)
                    last = pe.matmul(D(2)[:, ks], Qh[e][:, j * P:(j + 1) * P], Kh[e][:, ks], start=True, stop=True)
                last.then_inc(max_done, 1)

            def max_row(e, n):
                pe.wait_ge(max_taken, STEPS * (n + 1))
                pe.matmul(ps[0:TT, 4, 0:P], nmax[:, e, :], idt[:, :], start=True, stop=True).then_inc(row_done, 1)

            def scores(e, n, u, s, guarded=True):
                if u == 0:
                    pe.wait_ge(low_ready, 2 * (n + 1))
                    pe.wait_ge(q3_ready, n + 1)
                    pe.wait_ge(row_ready, n + 1)
                if guarded:
                    pe.wait_ge(probs_ready, 2 * s - 2)
                qs = slice(u // 4 * HALF, (u // 4 + 1) * HALF)
                for i in range(2):
                    kt = 2 * (u % 4) + i
                    ks = slice(kt * P, (kt + 1) * P)
                    out = D(u % 2)[:, i * HALF:(i + 1) * HALF]
                    pe.matmul(out, K3[e][:, ks], Q3[e][:, qs], start=True, stop=False)
                    pe.matmul(out, Kh[e][:, ks], Ql[e][:, qs], start=False, stop=False)
                    last = pe.matmul(out, Kh[e][:, ks], Qh[e][:, qs], start=False, stop=True)
                last.then_inc(sc_done, 1)

            def values(e, n, u, s):
                half = u // 4
                if u == 0:
                    pe.wait_ge(v0_ready, n + 1)
                if u % 4 == 0:
                    pe.wait_ge(out_taken, 2 * n + half + 1)
                    pe.wait_ge(sum_taken, 2 * n + half + 1)
                pe.wait_ge(lo_ready, s + 3)
                out = ps[:, 6 + half, :]
                for i in range(2):
                    kt = 2 * (u % 4) + i
                    cols = slice(i * HALF, (i + 1) * HALF)
                    pe.matmul(out, V1[e][:, kt, :], Pl[u % 2][:, cols], start=(u % 4 == 0 and i == 0), stop=False)
                    pe.matmul(out, V0[e][:, kt, :], Ph[u % 2][:, cols], start=False, stop=False)
                    last = pe.matmul(out, V1[e][:, kt, :], Ph[u % 2][:, cols], start=False, stop=(u % 4 == 3 and i == 1))
                last.then_inc(pv_done, 1)

            def pair(g, last_pair):
                for t in range(2 * STEPS):
                    e, u = t // STEPS, t % STEPS
                    n, s = 2 * g + e, 2 * STEPS * g + t
                    following = not (last_pair and e == 1)
                    if u == ROW_AT and following:
                        max_row(1 - e, n + 1)
                    if not (last_pair and t + AHEAD >= 2 * STEPS):
                        e2, u2 = (t + AHEAD) // STEPS % 2, (t + AHEAD) % STEPS
                        scores(e2, 2 * g + (t + AHEAD) // STEPS, u2, s + AHEAD)
                    tiles = MAX_AT.get(u, [])
                    ahead = 2 if u > ROW_AT else 1
                    if last_pair and e + ahead > 1:
                        tiles = []
                    early = tiles[:1] if u in MAX_FIRST else []
                    for j in early:
                        max_tile((e + ahead) % 2, n + ahead, j)
                    values(e, n, u, s)
                    for j in tiles[len(early):]:
                        max_tile((e + ahead) % 2, n + ahead, j)

            def transposes(n, c):
                if c == 0:
                    pe.wait_ge(x_loaded, 16 * (n + 1))
                if c >= 2:
                    pe.wait_ge(xt_ready, CT * n + c - 1)
                for t in range(TT):
                    last = pe.transpose(D(2 + c % 2)[:, t * P:(t + 1) * P], xin[:, t, c * P:(c + 1) * P], idt[:, :])
                last.then_inc(tr_done, 1)

            def group_sums(n, value):
                if value == 0:
                    pe.wait_ge(xt_ready, CT * (n + 1))
                    pe.wait_ge(aggr_ready, CT * (n + 1))
                else:
                    pe.wait_ge(norm_dve, 7 * n + 5)
                for c in range(CT):
                    moving = cvar[:, c:c + 1] if value else mv[:, c, 0:1]
                    last = pe.matmul(ps[0:GROUPS, 4 + 2 * value, 0:1], memb[:, c, :], moving, start=(c == 0), stop=(c == CT - 1))
                last.then_inc(norm_pe, 1)

            def group_spread(n, value):
                if value == 0:
                    pe.wait_ge(norm_dve, 7 * n + 1)
                else:
                    pe.wait_ge(norm_pool, n + 1)
                for c in range(CT):
                    last = pe.matmul(ps[:, 5 + 2 * value, c:c + 1], membt[:, c, :], gstat[:, 2 * value:2 * value + 1], start=True, stop=True)
                last.then_inc(norm_pe, 1)

            pe.wait_ge(consts, 64)
            for c in range(CT):
                transposes(0, c)
            for value in range(2):
                group_sums(0, value)
                group_spread(0, value)
            with pe.Fori(0, LAYERS * B) as lb:
                pe.wait_ge(y_evac, CT * lb + 1)

                def qk_tile(m):
                    if m % 2 == 0:
                        pe.wait_ge(ws_ready, CHUNKS * lb + m // 2 + 3)
                    last = transposed_weights_tile(m // 2 % 2, m % 2, D(m % 4), lb if m == 0 else None)
                    last.then_inc(mt_done, 1)

                for m in range(CT):
                    if m >= 4:
                        pe.wait_ge(mt_act, CT * lb + m - 3)
                        pe.wait_ge(mt_dve, 3 * CT * lb + 2 * (m - 3))
                    qk_tile(m)
                pe.wait_ge(mt_act, CT * (lb + 1))
                pe.wait_ge(mt_dve, 3 * CT * lb + 2 * CT)
                pe.wait_ge(tab_ready, 6 * (lb + 1))
                grid = qT.rearrange("p m (h w) -> p m h w", h=HW)
                for r in range(HW):
                    if r >= 8:
                        pe.wait_ge(rel_act, HW * lb + r - 7)
                        pe.wait_ge(rel_dve, HW * lb + r - 7)
                    for i in range(2):
                        at = 2 * (r % (HW // 2)) + i
                        back = HW - 1 - at
                        if r < HW // 2:
                            moving, table = grid[:, :, at, :], by_row[:, back, :]
                        else:
                            moving, table = grid[:, :, :, at], by_col[back // 24][:, back % 24, :]
                        M = table.shape[-1]
                        last = pe.matmul(ps[0:M, r % 8, i * CT * HW:(i + 1) * CT * HW].rearrange("p (m w) -> p m w", m=CT),
                                         table, moving, start=True, stop=True)
                    last.then_inc(rel_done, 1)
                pe.wait_ge(rel_act, HW * (lb + 1))
                pe.wait_ge(rel_dve, HW * (lb + 1))
                for m in range(CT, 2 * CT):
                    if m >= CT + 4:
                        pe.wait_ge(mt_dve, 3 * CT * lb + 2 * CT + m - CT - 3)
                    qk_tile(m)
                pe.wait_ge(mt_dve, 3 * CT * (lb + 1))
                for j in range(2 * CT // 2, QKV_CHUNKS):
                    pe.wait_ge(ws_ready, CHUNKS * lb + j + 3)
                    for t in range(TT):
                        d = 2 * (j - CT) + t // 4
                        if d >= 4 and t % 4 == 0:
                            pe.wait_ge(v_evac, CT * lb + d - 3)
                        last = token_tile(j % 2, t, D(d % 4)[:, t % 4 * WC:(t % 4 + 1) * WC])
                        if t % 4 == 3:
                            last.then_inc(v_done, 1)
                        if j == QKV_CHUNKS - 1:
                            if t == 0:
                                pe.wait_ge(v_evac, CT * lb + 3)
                            max_tile(0, HEADS * lb, t, guarded=False)
                n0 = HEADS * lb
                max_row(0, n0)
                pe.wait_ge(v_evac, CT * (lb + 1))
                pe.wait_ge(fill_dve, 8 * lb + 2)
                for u in range(AHEAD):
                    scores(0, n0, u, None, guarded=False)
                for u in (6, 7):
                    for j in MAX_AT[u]:
                        max_tile(1, n0 + 1, j)
                with pe.Fori(0, PAIRS - 1) as p:
                    pair(PAIRS * lb + p, False)
                pair(PAIRS * lb + PAIRS - 1, True)
                pe.wait_ge(as_ready, CT * (lb + 1))
                pe.wait_ge(probs_ready, 4 * STEPS * PAIRS * (lb + 1))
                pe.wait_ge(out_taken, 2 * HEADS * (lb + 1) + 2)
                pe.wait_ge(sum_taken, 2 * HEADS * (lb + 1) + 2)
                n = lb + 1
                between = {(0, 1): lambda: transposes(n, 0), (0, 3): lambda: transposes(n, 1),
                           (0, 5): lambda: transposes(n, 2), (0, 7): lambda: transposes(n, 3),
                           (1, 1): lambda: transposes(n, 4), (1, 3): lambda: transposes(n, 5),
                           (1, 5): lambda: group_sums(n, 0), (1, 7): lambda: group_spread(n, 0),
                           (2, 1): lambda: group_sums(n, 1), (2, 4): lambda: group_spread(n, 1)}
                for j in range(PROJ_CHUNKS):
                    pe.wait_ge(ws_ready, CHUNKS * lb + QKV_CHUNKS + j + 3)
                    for t in range(TT):
                        d = 2 * j + t // 4
                        if d >= 2 and t % 4 == 0:
                            pe.wait_ge(y_evac, CT * lb + d)
                        last = token_tile((QKV_CHUNKS + j) % 2, t, D(d % 2)[:, t % 4 * WC:(t % 4 + 1) * WC])
                        if t % 4 == 3:
                            last.then_inc(y_done, 1)
                        if (j, t) in between:
                            between[j, t]()

        @block.scalar
        def _(act):
            def copy(out, in_):
                return act.activation(out, in_, ACT.Copy)

            def w_high(n, j):
                act.wait_ge(w_loaded[j % 2], 16 * (CHUNKS // 2 * n + j // 2 + 1))
                copy(wsplit(j % 2, 0), wraw[:, j % 2, :, :]).then_inc(wh_ready, 1)

            def x_out(n, c):
                act.wait_ge(tr_done, CT * n + c + 1)
                copy(xT[:, c, :], D(2 + c % 2)).then_inc(xt_ready, 1)

            def key_high(e, pr):
                copy(Kh[e][own[e], :], k32[own[e], bass.ds(pr, 1), :].rearrange("p a s -> p (a s)")).then_inc(kh_ready, 1)

            def query_copy(e, pr):
                copy(Q3[e][own[e], :], qa[e][own[e], bass.ds(pr, 1), :].rearrange("p a s -> p (a s)")).then_inc(q3_ready, 1)

            def split_v(e, pr):
                copy(V1[e][:, :, own[e]], v32[:, :, bass.ds(pr * P + e * HD, HD)]).then_inc(v1_ready, 1)

            def exps(u, s):
                act.wait_ge(sc_done, s + 1)
                act.wait_ge(lo_ready, s + 1)
                act.activation(p32[:, u % 2, :], D(u % 2), ACT.Exp).then_inc(probs_ready, 1)
                act.wait_ge(pv_done, s + 1)
                act.activation(Ph[u % 2], D(u % 2), ACT.Exp).then_inc(probs_ready, 1)

            def out_half(e, pr, s, half):
                act.wait_ge(pv_done, s + 3)
                copy(attn[own[e], bass.ds(pr, 1), half * HALF:(half + 1) * HALF].rearrange("p a s -> p (a s)"),
                     ps[own[e], 6 + half, :]).then_inc(out_taken, 1)

            def attn_high(lb, c):
                act.wait_ge(an_ready, CT * lb + c + 1)
                copy(xh[c], attn[:, c, :]).then_inc(ah_ready, 1)

            def pair(lb, p, last_pair):
                g = PAIRS * lb + p
                for t in range(2 * STEPS):
                    e, u = t // STEPS, t % STEPS
                    n, s = 2 * g + e, 2 * STEPS * g + t
                    if not (last_pair and t + AHEAD >= 2 * STEPS):
                        exps((t + AHEAD) % STEPS, s + AHEAD)
                    if u % 4 == 3 and not last_pair:
                        out_half(e, p, s, u // 4)
                    if u == 1 and not (last_pair and e == 1):
                        act.wait_ge(pv_done, STEPS * n + 2)
                        split_v(1 - e, p + e)
                    if u == ROW_AT and not last_pair:
                        act.wait_ge(sc_done, STEPS * (n + 1))
                        key_high(e, p + 1)
                        query_copy(e, p + 1)
                    if last_pair and t == 8:
                        act.wait_ge(sc_done, STEPS * n)
                        w_high(lb, QKV_CHUNKS)
                    if last_pair and t in (12, 13):
                        act.wait_ge(pv_done, STEPS * n + 2)
                        attn_high(lb, t - 12)
                    if last_pair and t in (14, 15):
                        act.wait_ge(sc_done, STEPS * (n + 1))
                        attn_high(lb, t - 12)

            for c in range(CT):
                x_out(0, c)
            w_high(0, 0)
            with act.Fori(0, LAYERS * B) as lb:
                act.wait_ge(y_done, CT * lb + 1)
                for c in range(CT):
                    act.wait_ge(xn_ready, CT * lb + c + 1)
                    copy(xh[c], xT[:, c, :]).then_inc(xh_ready, 1)
                w_high(lb, 1)
                act.wait_ge(small, 32 * (lb + 1))
                act.wait_ge(tab_zero, 2 * (lb + 1))
                for e, at_row, at_col in ((0, 64, 96), (1, 0, 32)):
                    for dst, at, first in ((by_row, at_row, 0), (by_col[0], at_col, 0), (by_col[1], at_col, 24)):
                        kind, count = int(dst is not by_row), dst.shape[1]
                        copy(dst[own[e], :, at:at + HW], windows(e, kind, first, count)).then_inc(tab_ready, 1)
                for m in range(CT):
                    act.wait_ge(mt_done, 2 * CT * lb + m + 1)
                    if m == 0:
                        act.wait_ge(stored, 16 * lb + 16)
                    act.activation(qT[:, m, :], D(m % 4), ACT.Identity, bias=qkb[:, m:m + 1]).then_inc(mt_act, 1)
                    if m % 2:
                        w_high(lb, m // 2 + 2)
                for r in range(HW):
                    act.wait_ge(rel_done, HW * lb + r + 1)
                    rel_out(act.activation, ps, qa[1], r, 0, True).then_inc(rel_act, 1)
                for m in range(CT + 1, 2 * CT, 2):
                    act.wait_ge(mt_done, 2 * CT * lb + m + 1)
                    w_high(lb, m // 2 + 2)
                act.wait_ge(v_done, CT * lb + 2)
                w_high(lb, QKV_CHUNKS - 1)
                act.wait_ge(v_done, CT * lb + 4)
                copy(Kh[0][other[0], :], codes[HD:P, :])
                key_high(0, 0)
                act.wait_ge(v_done, CT * (lb + 1))
                query_copy(0, 0)
                act.wait_ge(v_evac, CT * (lb + 1))
                split_v(0, 0)
                copy(Kh[1][other[1], :], codes[HD:P, :])
                key_high(1, 0)
                exps(0, 2 * STEPS * PAIRS * lb)
                query_copy(1, 0)
                exps(1, 2 * STEPS * PAIRS * lb + 1)
                with act.Fori(0, PAIRS - 1) as p:
                    pair(lb, p, False)
                pair(lb, PAIRS - 1, True)
                act.wait_ge(pv_done, 2 * STEPS * PAIRS * (lb + 1) + 2)
                attn_high(lb, 4)
                w_high(lb, QKV_CHUNKS + 1)
                attn_high(lb, 5)
                for c in range(4):
                    x_out(lb + 1, c)
                act.wait_ge(y_done, CT * lb + 3)
                w_high(lb, QKV_CHUNKS + 2)
                for c in range(4, CT):
                    x_out(lb + 1, c)
                act.wait_ge(y_done, CT * lb + 5)
                w_high(lb + 1, 0)

        @block.vector
        def _(dve):
            for ring, free in ((ws_ready, 2), (lo_ready, 2), (pv_done, 2), (out_taken, 2), (sum_taken, 2),
                               (y_done, 1), (y_evac, 1), (stored, 16), (sum_stored[0], 16), (sum_stored[1], 16)):
                dve.sem_inc(ring, free)

            def max_take(e, n, j):
                dve.wait_ge(max_done, STEPS * n + j + 1)
                dve.tensor_reduce(nmax[:, e, j:j + 1], D(2), AX_X, ALU.max, negate=True).then_inc(max_taken, 1)

            def low(u, s):
                dve.wait_ge(probs_ready, 2 * (s + 1))
                dve.wait_ge(pv_done, s + 1)
                dve.tensor_tensor(Pl[u % 2], p32[:, u % 2, :], Ph[u % 2], ALU.subtract).then_inc(lo_ready, 1)

            def query_high(e, pr):
                dve.tensor_copy(Qh[e], qa[e][:, bass.ds(pr, 1), :].rearrange("p a s -> p (a s)")).then_inc(qh_ready, 1)

            def row(e, n):
                dve.wait_ge(row_done, n + 1)
                r = first_other[e]
                dve.tensor_tensor(Q3[e][r:r + TT, :].rearrange("p (t q) -> p t q", t=TT),
                                  ps[0:TT, 4:5, 0:P].to_broadcast([TT, TT, P]),
                                  codes[0:TT, :].rearrange("p (t q) -> p t q", t=TT), ALU.mult).then_inc(row_ready, 1)

            def sum_half(e, g, s, half):
                dve.wait_ge(pv_done, s + 3)
                if half == 0:
                    dve.wait_ge(sum_stored[e], 16 * g + 16)
                r = first_other[e]
                dve.tensor_copy(sumrow[r:r + 1, half * HALF:(half + 1) * HALF], ps[r:r + 1, 6 + half, :]).then_inc(sum_taken, 1)

            def norm_half(e, lb, s, half):
                cols = slice(half * HALF, (half + 1) * HALF)
                dve.wait_ge(pv_done, s + 3)
                for row_of in range(2):
                    dve.wait_ge(sum_stored[row_of], 16 * (PAIRS - 1) * (lb + 1) + 16)
                dve.reciprocal(sumrow[own[e], cols], ps[other[e], 6 + half, :]).then_inc(sum_taken, 1)
                dve.wait_ge(sum_taken, 2 * HEADS * lb + 2 * (HEADS - 2 + e) + half + 3)
                dve.tensor_tensor(attn[own[e], PAIRS - 1, cols], ps[own[e], 6 + half, :], sumrow[own[e], cols],
                                  ALU.mult).then_inc(out_taken, 1)

            def attn_norm(lb, c):
                dve.tensor_tensor(attn[:, c, :], attn[:, c, :], recip[:, c, :], ALU.mult).then_inc(an_ready, 1)

            def attn_low(lb, c):
                dve.wait_ge(ah_ready, CT * lb + c + 1)
                dve.tensor_tensor(xl[c], attn[:, c, :], xh[c], ALU.subtract).then_inc(as_ready, 1)

            def pair(lb, p, last_pair):
                g = PAIRS * lb + p
                for t in range(2 * STEPS):
                    e, u = t // STEPS, t % STEPS
                    n, s = 2 * g + e, 2 * STEPS * g + t
                    if u == ROW_AT and not (last_pair and e == 1):
                        row(1 - e, n + 1)
                    ahead = 2 if u > ROW_AT else 1
                    tiles = [] if last_pair and e + ahead > 1 else MAX_AT.get(u, [])
                    for j in tiles:
                        max_take((e + ahead) % 2, n + ahead, j)
                    if not (last_pair and t + AHEAD >= 2 * STEPS):
                        low((t + AHEAD) % STEPS, s + AHEAD)
                    if u % 4 == 3 and not last_pair:
                        sum_half(e, (PAIRS - 1) * lb + p, s, u // 4)
                    if u == ROW_AT and not last_pair:
                        dve.wait_ge(sc_done, STEPS * (n + 1))
                        query_high(e, p + 1)
                    if last_pair and t == 5:
                        dve.wait_ge(rs_loaded, 16 * (lb + 1))
                        dve.reciprocal(rs[:, :], rs[:, :]).then_inc(rs_ready, 1)
                    if last_pair and t >= 11:
                        if t == 11:
                            dve.wait_ge(recip_loaded, 32 * (lb + 1))
                        attn_norm(lb, t - 11)
                    if last_pair and t in (14, 15):
                        attn_low(lb, t - 14)
                    if last_pair and u % 4 == 3:
                        norm_half(e, lb, s, u // 4)

            def x_stats(n, c):
                dve.wait_ge(xt_ready, CT * n + c + 1)
                for half in range(2):
                    dve.bn_stats(stats[:, c, 6 * half:6 * half + 6], xT[:, c, half * HALF:(half + 1) * HALF]).then_inc(stat_ready, 1)

            def x_aggregate(n):
                dve.wait_ge(stat_ready, 2 * CT * (n + 1))
                dve.sem_inc(gate, 1)
                for c in range(CT):
                    dve.bn_aggr(mv[:, c, :], stats[:, c, :]).then_inc(aggr_ready, 1)

            def means_in(n):
                dve.wait_ge(norm_pe, 4 * n + 1)
                dve.tensor_copy(gstat[:, 0:1], ps[0:GROUPS, 4, 0:1]).then_inc(norm_dve, 1)

            def deviations(n):
                dve.wait_ge(norm_pe, 4 * n + 2)
                dve.tensor_copy(cmean[:, :], ps[:, 5, 0:CT]).then_inc(norm_dve, 1)
                dve.wait_ge(norm_dve, 7 * n + 2)
                dve.tensor_tensor(dev[:, :], mv[:, :, 0], cmean[:, :], ALU.subtract).then_inc(norm_dve, 1)
                dve.wait_ge(norm_dve, 7 * n + 3)
                dve.tensor_tensor(dev2[:, :], dev[:, :], dev[:, :], ALU.mult).then_inc(norm_dve, 1)
                dve.wait_ge(norm_dve, 7 * n + 4)
                dve.tensor_tensor(cvar[:, :], dev2[:, :], mv[:, :, 1], ALU.add).then_inc(norm_dve, 1)

            def variances_in(n):
                dve.wait_ge(norm_pe, 4 * n + 3)
                dve.tensor_scalar(gstat[:, 1:2], ps[0:GROUPS, 6, 0:1], EPS, None, ALU.add).then_inc(norm_dve, 1)

            def normalise(n):
                dve.wait_ge(norm_pe, 4 * n + 4)
                dve.tensor_copy(crstd[:, :], ps[:, 7, 0:CT]).then_inc(norm_dve, 1)
                dve.wait_ge(norm_dve, 7 * (n + 1))
                for c in range(CT):
                    dve.tensor_scalar(xT[:, c, :], xT[:, c, :], cmean[:, c:c + 1], crstd[:, c:c + 1],
                                      ALU.subtract, ALU.mult).then_inc(xn_ready, 1)

            def y_out(lb, d):
                dve.wait_ge(y_done, CT * lb + d + 2)
                t0, cols = d % 2 * 4, slice(d // 2 * WC, (d // 2 + 1) * WC)
                out = resid[:, t0:t0 + 4, cols]
                dve.tensor_tensor(out, D(d % 2).rearrange("p (t n) -> p t n", t=4), out, ALU.add).then_inc(y_evac, 1)

            for c in range(CT):
                x_stats(0, c)
            x_aggregate(0)
            means_in(0)
            deviations(0)
            variances_in(0)
            normalise(0)
            with dve.Fori(0, LAYERS * B) as lb:
                for c in range(CT):
                    dve.wait_ge(xh_ready, CT * lb + c + 1)
                    dve.tensor_tensor(xl[c], xT[:, c, :], xh[c], ALU.subtract).then_inc(xs_ready, 1)
                dve.wait_ge(small, 32 * (lb + 1))
                for m in range(CT):
                    dve.wait_ge(mt_act, CT * lb + m + 1)
                    if m == 0:
                        dve.wait_ge(xs_ready, CT * (lb + 1))
                    for e in range(2):
                        dve.tensor_scalar(qa[e][own[e], m, :], D(m % 4)[own[e], :], qkb[own[e], m:m + 1], None,
                                          ALU.add).then_inc(mt_dve, 1)
                for r in range(HW):
                    dve.wait_ge(rel_done, HW * lb + r + 1)
                    rel_out(dve.tensor_copy, ps, qa[0], r, HD, False).then_inc(rel_dve, 1)
                for m in range(CT):
                    dve.wait_ge(mt_done, 2 * CT * lb + CT + m + 1)
                    dve.tensor_scalar(k32[:, m, :], D((CT + m) % 4), qkb[:, CT + m:CT + m + 1], SCALE,
                                      ALU.add, ALU.mult).then_inc(mt_dve, 1)
                dve.wait_ge(rowb_loaded, 32 * lb + 16)

                def v_out(d):
                    dve.wait_ge(v_done, CT * lb + d + 1)
                    t0, cols = d % 2 * 4, slice(d // 2 * WC, (d // 2 + 1) * WC)
                    bias = rowb[:, cols].rearrange("p (a n) -> p a n", a=1).to_broadcast([P, 4, WC])
                    dve.tensor_tensor(v32[:, t0:t0 + 4, cols], D(d % 4).rearrange("p (t n) -> p t n", t=4), bias,
                                      ALU.add).then_inc(v_evac, 1)

                for d in range(4):
                    v_out(d)
                query_high(0, 0)
                for half in range(2):
                    for j in range(4):
                        max_take(0, HEADS * lb, 4 * half + j)
                    if half == 0:
                        v_out(4)
                dve.wait_ge(v_done, CT * (lb + 1))

                def fill(tile, value):
                    dve.memset(tile.bitcast(F32), value).then_inc(fill_dve, 1)

                fill(Q3[0][other[0], :], 0.0)
                fill(K3[0][other[0], :], 1.0)
                dve.wait_ge(fill_dve, 8 * lb + 1)
                row(0, HEADS * lb)
                v_out(5)
                query_high(1, 0)
                fill(V1[0][:, :, other[0]], 1.0)
                fill(V0[0][:, :, other[0]], 0.0)
                fill(Q3[1][other[1], :], 0.0)
                fill(K3[1][other[1], :], 1.0)
                fill(V1[1][:, :, other[1]], 1.0)
                fill(V0[1][:, :, other[1]], 0.0)
                for u in range(AHEAD):
                    low(u, 2 * STEPS * PAIRS * lb + u)
                for u in (6, 7):
                    for j in MAX_AT[u]:
                        max_take(1, HEADS * lb + 1, j)
                with dve.Fori(0, PAIRS - 1) as p:
                    pair(lb, p, False)
                pair(lb, PAIRS - 1, True)
                for c in range(2, CT):
                    if c == CT - 1:
                        dve.wait_ge(out_taken, 2 * HEADS * (lb + 1) + 2)
                        dve.sem_inc(an_ready, 1)
                    attn_low(lb, c)
                n = lb + 1
                dve.wait_ge(xb_ready, TT * (lb + 1))
                x_stats(n, 0)
                y_out(lb, 0)
                x_stats(n, 1)
                x_stats(n, 2)
                y_out(lb, 1)
                x_stats(n, 3)
                x_stats(n, 4)
                y_out(lb, 2)
                x_stats(n, 5)
                x_aggregate(n)
                means_in(n)
                y_out(lb, 3)
                deviations(n)
                variances_in(n)
                y_out(lb, 4)
                normalise(n)
                y_out(lb, 5)

        @block.gpsimd
        def _(pool):
            pool.memset(gstat[:, 3:4], -0.5).then_inc(primed, 1)
            pool.wait_ge(primed, 1)

            def w_low(lb, j):
                pool.wait_ge(wh_ready, CHUNKS * lb + j + 1)
                pool.tensor_tensor(wsplit(j % 2, 1), wraw[:, j % 2, :, :], wsplit(j % 2, 0), ALU.subtract).then_inc(ws_ready, 1)

            def split_qk(e, pr, n, v_tiles=None):
                pool.wait_ge(qh_ready, n + 1)
                pool.tensor_tensor(Ql[e], qa[e][:, bass.ds(pr, 1), :].rearrange("p a s -> p (a s)"), Qh[e],
                                   ALU.subtract).then_inc(low_ready, 1)
                pool.wait_ge(kh_ready, n + 1)
                if v_tiles is not None:
                    pool.wait_ge(v_done, v_tiles)
                pool.wait_ge(low_ready, 2 * n + 1)
                pool.tensor_tensor(K3[e][own[e], :], k32[own[e], bass.ds(pr, 1), :].rearrange("p a s -> p (a s)"),
                                   Kh[e][own[e], :], ALU.subtract).then_inc(low_ready, 1)
                pool.wait_ge(low_ready, 2 * (n + 1))
                pool.sem_inc(gate, 1)

            def split_v(e, pr, n):
                pool.wait_ge(v1_ready, n + 1)
                pool.tensor_tensor(V0[e][:, :, own[e]], v32[:, :, bass.ds(pr * P + e * HD, HD)], V1[e][:, :, own[e]],
                                   ALU.subtract).then_inc(v0_ready, 1)

            def inverse_deviation(n):
                pool.wait_ge(norm_dve, 7 * n + 6)
                pool.tensor_tensor(gstat[:, 2:3], gstat[:, 1:2], gstat[:, 3:4], ALU.pow).then_inc(norm_pool, 1)
                pool.wait_ge(norm_pool, n + 1)
                pool.sem_inc(gate, 1)

            w_low(0, 0)
            inverse_deviation(0)
            with pool.Fori(0, LAYERS * B) as lb:
                pool.wait_ge(y_done, CT * lb + 1)
                pool.sem_inc(gate, 1)
                pool.memset(k32_flat, 0.0).then_inc(tab_zero, 1)
                pool.memset(sumrow[:, :], 0.0).then_inc(tab_zero, 1)
                for j in range(1, QKV_CHUNKS):
                    w_low(lb, j)
                n0 = HEADS * lb
                split_qk(0, 0, n0, CT * (lb + 1))
                split_v(0, 0, n0)
                split_qk(1, 0, n0 + 1)
                with pool.Fori(0, PAIRS - 1) as p:
                    for e in range(2):
                        n = n0 + 2 * p + e
                        split_v(1 - e, p + e, n + 1)
                        split_qk(e, p + 1, n + 2)
                split_v(1, PAIRS - 1, n0 + HEADS - 1)
                pool.wait_ge(resid_loaded, 16 * (lb + 1))
                pool.wait_ge(rowb_loaded, 32 * (lb + 1))
                for t in range(TT):
                    pool.tensor_tensor(resid[:, t, :], resid[:, t, :], rowb[:, :], ALU.add).then_inc(xb_ready, 1)
                for j in range(QKV_CHUNKS, CHUNKS):
                    w_low(lb, j)
                inverse_deviation(lb + 1)
                w_low(lb + 1, 0)


def kernel(x, L0_conv_Wqkv, L0_conv_Wproj, L0_conv_bproj, L0_conv_rel_pos_h, L0_conv_rel_pos_w,
           L1_conv_qkv_w, L1_conv_qkv_b, L1_conv_proj_w, L1_conv_proj_b, L1_conv_rel_pos_h, L1_conv_rel_pos_w):
    import numpy as np
    import concourse.bacc as bacc
    from concourse.bass_utils import run_bass_kernel_spmd

    def f(a):
        return np.asarray(a)

    rel = np.zeros((LAYERS, P, 2, OFFS), np.float32)
    for l, (rh, rw) in enumerate(((L0_conv_rel_pos_h, L0_conv_rel_pos_w), (L1_conv_rel_pos_h, L1_conv_rel_pos_w))):
        for i, table in enumerate((rh, rw)):
            t = f(table)[:OFFS][::-1].T
            rel[l, :HD, i] = rel[l, HD:, i] = t
    qkv_b = np.stack([np.zeros(3 * C, np.float32), f(L1_conv_qkv_b)])
    tok = np.arange(S)
    code = np.zeros((P, S), np.float32)
    code[:TT] = np.arange(TT)[:, None] == tok // P
    code[HD:] = np.concatenate([np.arange(HW)[:, None] == tok // HW, np.arange(HW)[:, None] == tok % HW])
    group = np.arange(C) // (C // GROUPS)
    member = (group[:, None] == np.arange(GROUPS)).astype(np.float32)
    arrays = {
        "x": f(x).reshape(B, S, C),
        "wqkv": np.stack([f(L0_conv_Wqkv), f(L1_conv_qkv_w)]),
        "wproj": np.stack([f(L0_conv_Wproj), f(L1_conv_proj_w)]),
        "qk_bias": np.ascontiguousarray(qkv_b[:, :2 * C].reshape(LAYERS, 2 * CT, P).transpose(0, 2, 1)),
        "v_bias": np.ascontiguousarray(qkv_b[:, 2 * C:]),
        "proj_bias": np.stack([f(L0_conv_bproj), f(L1_conv_proj_b)]),
        "rel": rel,
        "code": code,
        "ident": np.eye(P, dtype=np.float32),
        "member": np.ascontiguousarray(member.reshape(CT, P, GROUPS).transpose(1, 0, 2)) / np.float32(C // GROUPS),
        "member_t": np.ascontiguousarray(member.T.reshape(GROUPS, CT, P)),
    }
    nc = bacc.Bacc("TRN2", target_bir_lowering=False, num_devices=1)
    ins = [nc.dram_tensor(f"in_{k}", a.shape, mybir.dt.from_np(a.dtype), kind="ExternalInput").ap() for k, a in arrays.items()]
    out = nc.dram_tensor("state", ((LAYERS + 1) * B, S, C), F32, kind="ExternalOutput").ap()
    two_layers(nc, *ins, out)
    r = run_bass_kernel_spmd(nc, [{f"in_{k}": a for k, a in arrays.items()}], core_ids=[0])
    return r.results[0]["state"][LAYERS * B:].reshape(B, HW, HW, C)
```

```python
from contextlib import ExitStack

import concourse.bass as bass
from concourse import mybir

F32 = mybir.dt.float32
F32R = mybir.dt.float32r
ALU = mybir.AluOpType
ACT = mybir.ActivationFunctionType
AX_X = mybir.AxisListType.X

P = 128
LAYERS, B, HW, C = 2, 4, 32, 768
S = HW * HW
HEADS, HD = 12, 64
PAIRS = HEADS // 2
CT = C // P
TT = S // P
GROUPS = 32
HALF = 512
WC = 256
QKV_CHUNKS, PROJ_CHUNKS = 3 * C // WC, C // WC
CHUNKS = QKV_CHUNKS + PROJ_CHUNKS
OFFS = 2 * HW - 1
SCALE = HD ** -0.5
EPS = 1e-5
FIRST_PIECES = 3
STEPS = 8
AHEAD = 2
ORDER = ["SSV2V", "SSV3V", "SS4VV", "S5SVV", "6SSVV7", "SSVRV", "VVSS0", "SSVV1"]
TAKES = [[2], [3], [4, 5], [6], [7], [], [0], [1]]
RECIPS = 2 * 16 * (PAIRS - 1) + 16
REL_BANKS = (0, 1, 2, 3, 6, 7)
FIRST_MAX = {(4, 1): (0, 1), (4, 2): (2,), (4, 3): (3, 4), (4, 4): (5,), (4, 5): (6,), (5, 0): (7,)}
V_PLACE = (0, 1, 2, 3, 0, 3)
ROW_AT = 5


def two_layers(nc, x, wqkv, wproj, qk_bias, v_bias, proj_bias, rel, code, ident, member, member_t,
               state):
    with ExitStack() as ctx:
        def sb(name, shape, dt=F32):
            return ctx.enter_context(nc.sbuf_tensor(name, shape, dt))

        def sem(name):
            return ctx.enter_context(nc.semaphore(name))

        sums_dram = nc.dram_tensor("sums_scratch", (LAYERS * B, HEADS, S), F32, kind="Internal").ap()
        recips_dram = nc.dram_tensor("recips_scratch", (LAYERS * B, HEADS, S), F32, kind="Internal").ap()

        qa = [sb("q_even", [P, CT, S]), sb("q_odd", [P, CT, S])]
        xT = qa[0]
        attn = qa[0]
        k32 = sb("k32", [P, CT, S])
        recip = k32
        v32 = sb("v32", [P, TT, C])
        resid = v32
        qT = v32[:, :, :].rearrange("p t c -> p (t c)").rearrange("p (m s) -> p m s", m=CT)
        wraw = sb("wraw", [P, 2, CT, WC])
        p32 = sb("p32", [P, 2, S])
        xin = qa[1][:, :, :].rearrange("p m s -> p (m s)").rearrange("p (t c) -> p t c", t=TT)
        sumrow = sb("sumrow", [P, S])
        codes = sb("codes", [P, S])
        idt = sb("idt", [P, P])
        tab = sb("tab", [P, 2, OFFS])
        qkb = sb("qkb", [P, 2 * CT])
        rowb = sb("rowb", [P, C])
        memb = sb("memb", [P, CT, GROUPS])
        membt = sb("membt", [GROUPS, CT, P])
        stats = sb("stats", [P, CT, 12])
        mv = sb("mv", [P, CT, 2])
        gstat = sb("gstat", [GROUPS, 4])
        cmean = sb("cmean", [P, CT])
        crstd = sb("crstd", [P, CT])
        dev = sb("dev", [P, CT])
        dev2 = sb("dev2", [P, CT])
        cvar = sb("cvar", [P, CT])
        nmax = sb("nmax", [P, 2, TT])
        rs = sb("rs", [P, 2 * S // P])

        k32_flat = k32[:, :, :].rearrange("p m s -> p (m s)")
        by_row = k32_flat[:, 0:HW * 96].rearrange("p (a n) -> p a n", n=96)
        by_col = [k32_flat[:, HW * 96:].rearrange("p (a n) -> p a n", n=P),
                  sumrow[:, :].rearrange("p (a n) -> p a n", n=P)]

        def windows(e, kind, first, count):
            base = tab[own[e], kind, first:first + 1]
            return bass.AP(tensor=base.tensor, offset=base.offset, ap=[list(base.ap[0]), [1, count], [1, HW]])

        R = sb("R", [P, 18 * S], F32R)

        def rtile(i):
            return R[:, i * S:(i + 1) * S]

        Qh, Kh, Ql, Q3, K3 = ([rtile(7 * e + i) for e in range(2)] for i in range(5))
        V1, V0 = ([rtile(7 * e + i).rearrange("p (t m) -> p t m", t=TT) for e in range(2)] for i in (5, 6))
        Ph = [rtile(14), rtile(15)]
        Pl = [rtile(16), rtile(17)]
        xh = [rtile(3 + 2 * k) for k in range(CT)]
        xl = [rtile(4 + 2 * k) for k in range(CT)]

        def wsplit(slot, low):
            o = (0 if slot else 15 * S) + low * CT * WC
            return R[:, o:o + CT * WC].rearrange("p (k n) -> p k n", k=CT)

        own = [slice(0, HD), slice(HD, P)]
        other = [slice(HD, P), slice(0, HD)]
        first_other = [HD, 0]

        ps = ctx.enter_context(nc.psum_tensor("ps", [P, 8, HALF], F32))

        def D(i):
            return ps[:, 2 * i:2 * i + 2, :].rearrange("p a n -> p (a n)")

        consts = sem("consts")
        small = sem("small")
        rowb_loaded = sem("rowb_loaded")
        first_loaded = [sem("first_loaded%d" % j) for j in range(FIRST_PIECES)]
        x_loaded = sem("x_loaded")
        resid_loaded = sem("resid_loaded")
        copied = sem("copied")
        w_loaded = [sem("w_loaded0"), sem("w_loaded1")]
        primed = sem("primed")
        gate = sem("gate")
        tab_zero = sem("tab_zero")
        tab_ready = sem("tab_ready")
        tr_done = sem("tr_done")
        xt_ready = sem("xt_ready")
        stat_ready = sem("stat_ready")
        aggr_ready = sem("aggr_ready")
        norm_pe = sem("norm_pe")
        norm_dve = sem("norm_dve")
        norm_pool = sem("norm_pool")
        xn_ready = sem("xn_ready")
        xh_ready = sem("xh_ready")
        xs_ready = sem("xs_ready")
        wh_ready = sem("wh_ready")
        ws_ready = sem("ws_ready")
        mt_done = sem("mt_done")
        mt_act = sem("mt_act")
        mt_dve = sem("mt_dve")
        rel_done = sem("rel_done")
        rel_act = sem("rel_act")
        rel_dve = sem("rel_dve")
        v_done = sem("v_done")
        v_evac = sem("v_evac")
        code_ready = sem("code_ready")
        fill_dve = sem("fill_dve")
        fill_pool = sem("fill_pool")
        qh_ready = sem("qh_ready")
        kh_ready = sem("kh_ready")
        q3_ready = sem("q3_ready")
        low_ready = sem("low_ready")
        v1_ready = sem("v1_ready")
        v0_ready = sem("v0_ready")
        max_done = sem("max_done")
        max_taken = sem("max_taken")
        row_done = sem("row_done")
        row_ready = sem("row_ready")
        sc_done = sem("sc_done")
        probs_ready = sem("probs_ready")
        lo_ready = sem("lo_ready")
        pv_done = sem("pv_done")
        out_taken = sem("out_taken")
        sum_taken = sem("sum_taken")
        sum_stored = [sem("sum_stored0"), sem("sum_stored1")]
        rs_loaded = sem("rs_loaded")
        rs_ready = sem("rs_ready")
        rs_stored = sem("rs_stored")
        recip_loaded = sem("recip_loaded")
        an_ready = sem("an_ready")
        ah_ready = sem("ah_ready")
        al_pool = sem("al_pool")
        al_dve = sem("al_dve")
        v_dead = sem("v_dead")
        y_dead = sem("y_dead")
        xb_ready = sem("xb_ready")
        y_done = sem("y_done")
        y_evac = sem("y_evac")
        stored = sem("stored")

        block = ctx.enter_context(nc.Block())

        def rel_out(op, ps, dst, r, base, on_act):
            at = 2 * (r % (HW // 2))
            by_row = r < HW // 2
            q = base + (0 if by_row else HW)
            grid = dst[q:q + HW, :, :].rearrange("p m (h w) -> p m h w", h=HW)
            if by_row:
                out = grid[:, :, at:at + 2, :].rearrange("p m a w -> p a m w")
            else:
                out = grid[:, :, :, at:at + 2].rearrange("p m h a -> p a m h")
            in_ = ps[q:q + HW, REL_BANKS[r % len(REL_BANKS)], 0:2 * CT * HW].rearrange("p (a m w) -> p a m w", a=2, m=CT)
            return op(out, in_, ACT.Copy) if on_act else op(out, in_)

        @block.sync
        def _(sp):
            for dst, src in ((idt, ident), (codes, code), (memb, member), (membt, member_t)):
                sp.dma_start(dst[tuple([slice(None)] * len(dst.shape))], src).then_inc(consts, 16)
            for j in range(FIRST_PIECES):
                cols = slice(j * C // FIRST_PIECES, (j + 1) * C // FIRST_PIECES)
                sp.dma_start(xin[:, :, cols], x[0, :, cols].rearrange("(t p) c -> p t c", p=P)).then_inc(first_loaded[j], 16)

            def load_chunk(n, layer, j):
                sp.wait_ge(ws_ready, CHUNKS * n + j + 1)
                sp.sem_inc(gate, 1)
                w, c0 = (wqkv, j * WC) if j < QKV_CHUNKS else (wproj, (j - QKV_CHUNKS) * WC)
                src = w[bass.ds(layer, 1), :, c0:c0 + WC].rearrange("a (k p) n -> p (a k) n", p=P)
                sp.dma_start(wraw[:, j % 2, :, :], src).then_inc(w_loaded[j % 2], 16)

            load_chunk(0, 0, 0)
            load_chunk(0, 0, 1)
            sp.dma_start(state[0:B], x).then_inc(copied, 16)

            with sp.Fori(0, LAYERS * B) as lb:
                layer = lb // B
                sp.dma_start(tab[:, :, :], rel[bass.ds(layer, 1)].rearrange("a p r n -> p (a r) n")).then_inc(small, 16)
                sp.dma_start(qkb[:, :], qk_bias[bass.ds(layer, 1)].rearrange("a p m -> p (a m)")).then_inc(small, 16)
                sp.dma_start(rowb[:, :], v_bias[bass.ds(layer, 1)].to_broadcast([P, C])).then_inc(rowb_loaded, 16)
                for j in range(2, QKV_CHUNKS):
                    load_chunk(lb, layer, j)
                sp.wait_ge(v_evac, CT * (lb + 1))
                sp.sem_inc(gate, 1)
                sp.dma_start(rowb[:, :], proj_bias[bass.ds(layer, 1)].to_broadcast([P, C])).then_inc(rowb_loaded, 16)
                load_chunk(lb, layer, QKV_CHUNKS)
                load_chunk(lb, layer, QKV_CHUNKS + 1)

                with sp.Fori(0, PAIRS - 1) as p:
                    for e in range(2):
                        sp.wait_ge(sum_taken, 2 * (2 * (PAIRS * lb + p) + e) + 4)
                        sp.sem_inc(gate, 1)
                        r = first_other[e]
                        sp.dma_start(sums_dram[bass.ds(lb, 1), bass.ds(2 * p + e, 1), :].rearrange("a h s -> (a h) s"),
                                     sumrow[r:r + 1, :]).then_inc(sum_stored[e], 16)
                    for e in range(2):
                        sp.wait_ge(sum_stored[e], 16 * ((PAIRS - e) * lb + p) + 32)
                        sp.sem_inc(gate, 1)
                    sp.dma_start(rs[:, :], sums_dram[bass.ds(lb, 1), bass.ds(2 * p, 2)].rearrange("a h s -> (a h s)").rearrange("(p n) -> p n", p=P)).then_inc(rs_loaded, 16)
                    sp.wait_ge(rs_ready, PAIRS * lb + p + 1)
                    sp.sem_inc(gate, 1)
                    sp.dma_start(recips_dram[bass.ds(lb, 1), bass.ds(2 * p, 2)].rearrange("a h s -> (a h s)").rearrange("(p n) -> p n", p=P), rs[:, :]).then_inc(rs_stored, 16)
                    sp.wait_ge(rs_stored, 16 * (PAIRS * lb + p + 1))
                    sp.sem_inc(gate, 1)
                    for e in range(2):
                        src = recips_dram[bass.ds(lb, 1), bass.ds(2 * p + e, 1), :].rearrange("a h s -> (a h) s").to_broadcast([HD, S])
                        sp.dma_start(recip[own[e], bass.ds(p, 1), :].rearrange("p a s -> p (a s)"), src).then_inc(recip_loaded, 16)
                h = HEADS - 2
                sp.wait_ge(sum_taken, 2 * (HEADS * lb + h) + 4)
                sp.sem_inc(gate, 1)
                sp.dma_start(sums_dram[bass.ds(lb, 1), h], sumrow[HD:HD + 1, :]).then_inc(sum_stored[0], 16)
                sp.wait_ge(sum_stored[0], 16 * PAIRS * (lb + 1) + 16)
                sp.sem_inc(gate, 1)
                sp.dma_start(rs[:, 0:S // P], sums_dram[bass.ds(lb, 1), h].rearrange("a s -> (a s)").rearrange("(p n) -> p n", p=P)).then_inc(rs_loaded, 16)
                sp.wait_ge(rs_ready, PAIRS * (lb + 1))
                sp.sem_inc(gate, 1)
                sp.dma_start(recips_dram[bass.ds(lb, 1), h].rearrange("a s -> (a s)").rearrange("(p n) -> p n", p=P), rs[:, 0:S // P]).then_inc(rs_stored, 16)
                sp.wait_ge(rs_stored, 16 * PAIRS * (lb + 1))
                sp.sem_inc(gate, 1)
                sp.dma_start(sumrow[own[0], :], recips_dram[bass.ds(lb, 1), h].to_broadcast([HD, S])).then_inc(recip_loaded, 16)
                load_chunk(lb, layer, QKV_CHUNKS + 2)
                following = (lb + 1) % (LAYERS * B) // B
                load_chunk(lb + 1, following, 0)
                load_chunk(lb + 1, following, 1)
                for j in range(PROJ_CHUNKS):
                    sp.wait_ge(y_evac, CT * lb + 2 * j + 4)
                    sp.sem_inc(gate, 1)
                    cols = slice(j * WC, (j + 1) * WC)
                    sp.dma_start(state[bass.ds(lb + B, 1), :, cols].rearrange("a (t p) c -> p (a t) c", p=P),
                                 resid[:, :, cols]).then_inc(stored, 16)
            sp.wait_ge(stored, 16 * PROJ_CHUNKS * LAYERS * B + 16)
            sp.sem_inc(gate, 1)

        @block.tensor
        def _(pe):
            def three(out, a, b, first, last):
                pe.matmul(out, a[0], b[0], start=first, stop=False)
                pe.matmul(out, a[0], b[1], start=False, stop=False)
                return pe.matmul(out, a[1], b[0], start=False, stop=last)

            def transposed_weights_tile(slot, m, dst, image):
                cols = slice(m * P, (m + 1) * P)
                for half in range(2):
                    toks = slice(half * HALF, (half + 1) * HALF)
                    for k in range(CT):
                        if image is not None and half == 0:
                            pe.wait_ge(xs_ready, CT * image + k + 1)
                        last = three(dst[:, toks], (wsplit(slot, 0)[:, k, cols], wsplit(slot, 1)[:, k, cols]),
                                     (xh[k][:, toks], xl[k][:, toks]), k == 0, k == CT - 1)
                return last

            def token_group(slot, half, k, dst):
                for i in range(4):
                    toks = slice((4 * half + i) * P, (4 * half + i + 1) * P)
                    last = three(dst[:, i * WC:(i + 1) * WC], (xh[k][:, toks], xl[k][:, toks]),
                                 (wsplit(slot, 0)[:, k, :], wsplit(slot, 1)[:, k, :]),
                                 k == 0 and i % 2 == 0, k == CT - 1 and i % 2 == 1)
                return last

            def max_tile(e, n, j, first=False):
                if j == 0:
                    pe.wait_ge(qh_ready, n + 1)
                    pe.wait_ge(kh_ready, n + 1)
                    if not first:
                        pe.wait_ge(row_ready, n)
                elif not first:
                    pe.wait_ge(max_taken, STEPS * n + j)
                elif j >= 2:
                    pe.wait_ge(max_taken, STEPS * n + j - 1)
                dst = D(1) if first and j % 2 else D(2)
                for half in range(2):
                    ks = slice(half * HALF, (half + 1) * HALF)
                    last = pe.matmul(dst[:, ks], Qh[e][:, j * P:(j + 1) * P], Kh[e][:, ks], start=True, stop=True)
                last.then_inc(max_done, 1)

            def max_row(e, n):
                pe.wait_ge(max_taken, STEPS * (n + 1))
                pe.matmul(ps[0:TT, 4, 0:P], nmax[:, e, :], idt[:, :], start=True, stop=True).then_inc(row_done, 1)

            def scores(e, n, u, s, i, guarded=True):
                if i == 0 and u == 0:
                    pe.wait_ge(low_ready, 2 * (n + 1))
                    pe.wait_ge(q3_ready, n + 1)
                    pe.wait_ge(row_ready, n + 1)
                if i == 0 and guarded:
                    pe.wait_ge(probs_ready, 2 * s - 2)
                qs = slice(u // 4 * HALF, (u // 4 + 1) * HALF)
                kt = 2 * (u % 4) + i
                ks = slice(kt * P, (kt + 1) * P)
                out = D(u % 2)[:, i * HALF:(i + 1) * HALF]
                pe.matmul(out, K3[e][:, ks], Q3[e][:, qs], start=True, stop=False)
                pe.matmul(out, Kh[e][:, ks], Ql[e][:, qs], start=False, stop=False)
                last = pe.matmul(out, Kh[e][:, ks], Qh[e][:, qs], start=False, stop=True)
                if i == 1:
                    last.then_inc(sc_done, 1)

            def values(e, n, u, s, i):
                half = u // 4
                if i == 0:
                    if u == 0:
                        pe.wait_ge(v0_ready, n + 1)
                    if u % 4 == 0:
                        pe.wait_ge(out_taken, 2 * n + half + 1)
                        pe.wait_ge(sum_taken, 2 * n + half + 1)
                    pe.wait_ge(lo_ready, s + 3)
                out = ps[:, 6 + half, :]
                kt = 2 * (u % 4) + i
                cols = slice(i * HALF, (i + 1) * HALF)
                pe.matmul(out, V1[e][:, kt, :], Pl[u % 2][:, cols], start=(u % 4 == 0 and i == 0), stop=False)
                pe.matmul(out, V0[e][:, kt, :], Ph[u % 2][:, cols], start=False, stop=False)
                last = pe.matmul(out, V1[e][:, kt, :], Ph[u % 2][:, cols], start=False, stop=(u % 4 == 3 and i == 1))
                if i == 1:
                    last.then_inc(pv_done, 1)

            def pair(g, last_pair):
                for t in range(2 * STEPS):
                    e, u = t // STEPS, t % STEPS
                    n, s = 2 * g + e, 2 * STEPS * g + t
                    ahead = 2 if u > ROW_AT else 1
                    parts = {"S": 0, "V": 0}
                    for what in ORDER[u]:
                        if what == "V":
                            values(e, n, u, s, parts["V"])
                        elif what == "S":
                            if not (last_pair and t + AHEAD >= 2 * STEPS):
                                scores((t + AHEAD) // STEPS % 2, 2 * g + (t + AHEAD) // STEPS, (t + AHEAD) % STEPS,
                                       s + AHEAD, parts["S"])
                        elif last_pair and e + ahead > 1:
                            continue
                        elif what == "R":
                            max_row(1 - e, n + 1)
                        else:
                            max_tile((e + ahead) % 2, n + ahead, int(what))
                        if what in parts:
                            parts[what] += 1

            def transposes(n, c, after_attention=True):
                if after_attention and c == 0:
                    pe.wait_ge(x_loaded, 16 * n)
                if not after_attention:
                    pe.wait_ge(first_loaded[c * FIRST_PIECES // CT], 16)
                if c == 1 and after_attention:
                    pe.wait_ge(out_taken, 2 * HEADS * n + 2)
                    pe.wait_ge(sum_taken, 2 * HEADS * n + 2)
                if c >= 2:
                    pe.wait_ge(xt_ready, CT * n + c - 1)
                for t in range(TT):
                    last = pe.transpose(D(2 + c % 2)[:, t * P:(t + 1) * P], xin[:, t, c * P:(c + 1) * P], idt[:, :])
                last.then_inc(tr_done, 1)

            def group_sums(n, value):
                if value == 0:
                    pe.wait_ge(xt_ready, CT * (n + 1))
                    pe.wait_ge(aggr_ready, CT * (n + 1))
                else:
                    pe.wait_ge(norm_dve, 7 * n + 5)
                for c in range(CT):
                    moving = cvar[:, c:c + 1] if value else mv[:, c, 0:1]
                    last = pe.matmul(ps[0:GROUPS, 4 + 2 * value, 0:1], memb[:, c, :], moving, start=(c == 0), stop=(c == CT - 1))
                last.then_inc(norm_pe, 1)

            def group_spread(n, value):
                if value == 0:
                    pe.wait_ge(norm_dve, 7 * n + 1)
                else:
                    pe.wait_ge(norm_pool, n + 1)
                for c in range(CT):
                    last = pe.matmul(ps[:, 5 + 2 * value, c:c + 1], membt[:, c, :], gstat[:, 2 * value:2 * value + 1], start=True, stop=True)
                last.then_inc(norm_pe, 1)

            pe.wait_ge(consts, 64)
            for c in range(CT):
                transposes(0, c, after_attention=False)
            for value in range(2):
                group_sums(0, value)
                group_spread(0, value)
            with pe.Fori(0, LAYERS * B) as lb:

                def qk_tile(m):
                    if m % 2 == 0:
                        pe.wait_ge(ws_ready, CHUNKS * lb + m // 2 + 3)
                    last = transposed_weights_tile(m // 2 % 2, m % 2, D(m % 4), lb if m == 0 else None)
                    last.then_inc(mt_done, 1)

                for m in range(CT):
                    if m < 2:
                        pe.wait_ge(y_evac, CT * lb + m + 1)
                    if m >= 4:
                        pe.wait_ge(mt_act, CT * lb + m - 3)
                        pe.wait_ge(mt_dve, 3 * CT * lb + 2 * (m - 3))
                    qk_tile(m)
                pe.wait_ge(mt_act, CT * lb + CT - 3)
                pe.wait_ge(mt_dve, 3 * CT * lb + 2 * (CT - 3))
                qk_tile(CT)
                pe.wait_ge(mt_act, CT * (lb + 1))
                pe.wait_ge(mt_dve, 3 * CT * lb + 2 * CT)
                pe.wait_ge(tab_ready, 6 * (lb + 1))
                grid = qT.rearrange("p m (h w) -> p m h w", h=HW)
                for r in range(HW):
                    if r >= len(REL_BANKS):
                        pe.wait_ge(rel_act, HW * lb + r - len(REL_BANKS) + 1)
                        pe.wait_ge(rel_dve, HW * lb + r - len(REL_BANKS) + 1)
                    for i in range(2):
                        at = 2 * (r % (HW // 2)) + i
                        back = HW - 1 - at
                        if r < HW // 2:
                            moving, table = grid[:, :, at, :], by_row[:, back, :]
                        else:
                            moving, table = grid[:, :, :, at], by_col[back // 24][:, back % 24, :]
                        M = table.shape[-1]
                        last = pe.matmul(ps[0:M, REL_BANKS[r % len(REL_BANKS)], i * CT * HW:(i + 1) * CT * HW].rearrange("p (m w) -> p m w", m=CT),
                                         table, moving, start=True, stop=True)
                    last.then_inc(rel_done, 1)
                for m in range(CT + 1, 2 * CT):
                    if m <= CT + 2:
                        left = HW - 2 if m == CT + 1 else HW
                        pe.wait_ge(rel_act, HW * lb + left)
                        pe.wait_ge(rel_dve, HW * lb + left)
                    if m >= CT + 4:
                        pe.wait_ge(mt_dve, 3 * CT * lb + 2 * CT + m - CT - 3)
                    qk_tile(m)
                n0 = HEADS * lb
                for j in range(CT, QKV_CHUNKS):
                    pe.wait_ge(ws_ready, CHUNKS * lb + j + 3)
                    for half in range(2):
                        d = 2 * (j - CT) + half
                        if d < 4:
                            pe.wait_ge(mt_dve, 3 * CT * lb + 3 * CT - 3 + d)
                        else:
                            pe.wait_ge(v_evac, CT * lb + (1 if d == 4 else 4))
                        for k in range(CT):
                            last = token_group(j % 2, half, k, D(V_PLACE[d]))
                            if d == CT - 1:
                                last.then_inc(v_dead, 1)
                            elif k == CT - 1:
                                last.then_inc(v_done, 1)
                            if (d, k) == (4, 1):
                                pe.wait_ge(v_evac, CT * lb + 3)
                            for tile in FIRST_MAX.get((d, k), ()):
                                max_tile(0, n0, tile, first=True)
                            if (d, k) == (5, 2):
                                max_row(0, n0)
                pe.wait_ge(fill_dve, 4 * lb + 2)
                for u in range(AHEAD):
                    for i in range(2):
                        scores(0, n0, u, None, i, guarded=False)
                        if u == 1:
                            max_tile(1, n0 + 1, i)
                pe.wait_ge(v_evac, CT * (lb + 1))
                pe.sem_inc(gate, 1)
                with pe.Fori(0, PAIRS - 1) as p:
                    pair(PAIRS * lb + p, False)
                pair(PAIRS * lb + PAIRS - 1, True)
                pe.wait_ge(probs_ready, 4 * STEPS * PAIRS * (lb + 1))
                n = lb + 1
                between = {(0, 3): lambda: transposes(n, 0), (1, 2): lambda: transposes(n, 1),
                           (1, 3): lambda: transposes(n, 2), (1, 4): lambda: transposes(n, 3),
                           (1, 5): lambda: transposes(n, 4), (2, 0): lambda: transposes(n, 5),
                           (2, 4): lambda: group_sums(n, 0), (3, 0): lambda: group_spread(n, 0),
                           (3, 2): lambda: group_sums(n, 1), (3, 5): lambda: group_spread(n, 1)}
                for d in range(CT):
                    j, half = QKV_CHUNKS + d // 2, d % 2
                    if half == 0:
                        pe.wait_ge(ws_ready, CHUNKS * lb + j + 3)
                    if d >= 2:
                        pe.wait_ge(y_evac, CT * lb + d + 1)
                    for k in range(CT):
                        if d == 0 and k == 0:
                            pe.wait_ge(al_pool, 2 * (lb + 1))
                        if d == 0 and k >= 2:
                            pe.wait_ge(al_dve, 5 * lb + k - 1)
                        if d == 1 and k == CT - 1:
                            pe.wait_ge(al_dve, 5 * (lb + 1))
                        last = token_group(j % 2, half, k, D(half))
                        if d == CT - 1:
                            last.then_inc(y_dead, 1)
                        elif k == CT - 1:
                            last.then_inc(y_done, 1)
                        if (d, k) in between:
                            between[d, k]()

        @block.scalar
        def _(act):
            def copy(out, in_):
                return act.activation(out, in_, ACT.Copy)

            def w_high(n, j):
                act.wait_ge(w_loaded[j % 2], 16 * (CHUNKS // 2 * n + j // 2 + 1))
                copy(wsplit(j % 2, 0), wraw[:, j % 2, :, :]).then_inc(wh_ready, 1)

            def x_out(n, c):
                act.wait_ge(tr_done, CT * n + c + 1)
                copy(xT[:, c, :], D(2 + c % 2)).then_inc(xt_ready, 1)

            def key_high(e, pr):
                copy(Kh[e][own[e], :], k32[own[e], bass.ds(pr, 1), :].rearrange("p a s -> p (a s)")).then_inc(kh_ready, 1)

            def query_copy(e, pr):
                copy(Q3[e][own[e], :], qa[e][own[e], bass.ds(pr, 1), :].rearrange("p a s -> p (a s)")).then_inc(q3_ready, 1)

            def split_v(e, pr):
                copy(V1[e][:, :, own[e]], v32[:, :, bass.ds(pr * P + e * HD, HD)]).then_inc(v1_ready, 1)

            def exps(u, s):
                act.wait_ge(sc_done, s + 1)
                act.wait_ge(lo_ready, s + 1)
                act.activation(p32[:, u % 2, :], D(u % 2), ACT.Exp).then_inc(probs_ready, 1)
                act.wait_ge(pv_done, s + 1)
                act.activation(Ph[u % 2], D(u % 2), ACT.Exp).then_inc(probs_ready, 1)

            def out_half(e, pr, s, half):
                act.wait_ge(pv_done, s + 3)
                copy(attn[own[e], bass.ds(pr, 1), half * HALF:(half + 1) * HALF].rearrange("p a s -> p (a s)"),
                     ps[own[e], 6 + half, :]).then_inc(out_taken, 1)

            def attn_high(c, toks=slice(None)):
                copy(xh[c][:, toks], attn[:, c, toks]).then_inc(ah_ready, 1)

            def x_high(n, k):
                act.wait_ge(xn_ready, CT * n + k + 1)
                copy(xh[k], xT[:, k, :]).then_inc(xh_ready, 1)

            def pair(lb, p, last_pair):
                g = PAIRS * lb + p
                for t in range(2 * STEPS):
                    e, u = t // STEPS, t % STEPS
                    n, s = 2 * g + e, 2 * STEPS * g + t
                    if not (last_pair and t + AHEAD >= 2 * STEPS):
                        exps((t + AHEAD) % STEPS, s + AHEAD)
                    if u % 4 == 3 and not (last_pair and e == 1):
                        out_half(e, p, s, u // 4)
                    if u == 1 and not (last_pair and e == 1):
                        act.wait_ge(pv_done, STEPS * n + 2)
                        split_v(1 - e, p + e)
                    if u == ROW_AT and not last_pair:
                        act.wait_ge(sc_done, STEPS * (n + 1))
                        key_high(e, p + 1)
                    if u == 2 and not (last_pair and e == 1):
                        act.wait_ge(sc_done, STEPS * n)
                        query_copy(1 - e, p + e)
                    if last_pair and t == 3:
                        act.wait_ge(q3_ready, HEADS * (lb + 1))
                        act.wait_ge(low_ready, 2 * HEADS * (lb + 1))
                        act.wait_ge(copied, 16)
                        act.dma_start(xin, state[bass.ds(lb + 1, 1)].rearrange("a (t p) c -> p (a t) c", p=P)).then_inc(x_loaded, 16)
                        act.wait_ge(v0_ready, HEADS * (lb + 1))
                        act.dma_start(resid[:, :, :], state[bass.ds(lb, 1)].rearrange("a (t p) c -> p (a t) c", p=P)).then_inc(resid_loaded, 16)
                    if last_pair and t == 7:
                        act.wait_ge(sc_done, STEPS * (n + 1))
                        act.wait_ge(an_ready, PAIRS * lb + 4)
                        attn_high(0)
                    if last_pair and t == 10:
                        w_high(lb, QKV_CHUNKS)
                    if last_pair and t == 9:
                        act.wait_ge(pv_done, STEPS * n + 2)
                        attn_high(1)
                    if last_pair and t in (14, 15):
                        act.wait_ge(sc_done, STEPS * (n + 1))
                        attn_high(t - 12)

            for c in range(CT):
                x_out(0, c)
            w_high(0, 0)
            for k in range(CT):
                x_high(0, k)
            with act.Fori(0, LAYERS * B) as lb:
                act.wait_ge(y_dead, CT * lb + 1)
                w_high(lb, 1)
                act.wait_ge(small, 32 * (lb + 1))
                act.wait_ge(tab_zero, 2 * (lb + 1))
                for e, at_row, at_col in ((0, 64, 96), (1, 0, 32)):
                    for dst, at, first in ((by_row, at_row, 0), (by_col[0], at_col, 0), (by_col[1], at_col, 24)):
                        kind, count = int(dst is not by_row), dst.shape[1]
                        copy(dst[own[e], :, at:at + HW], windows(e, kind, first, count)).then_inc(tab_ready, 1)
                for m in range(CT):
                    act.wait_ge(mt_done, 2 * CT * lb + m + 1)
                    if m == 0:
                        act.wait_ge(stored, 16 * PROJ_CHUNKS * lb + 16)
                    act.activation(qT[:, m, :], D(m % 4), ACT.Identity, bias=qkb[:, m:m + 1]).then_inc(mt_act, 1)
                    if m % 2:
                        w_high(lb, m // 2 + 2)
                for r in range(HW):
                    act.wait_ge(rel_done, HW * lb + r + 1)
                    rel_out(act.activation, ps, qa[1], r, 0, True).then_inc(rel_act, 1)
                for m in range(CT + 1, 2 * CT, 2):
                    act.wait_ge(mt_done, 2 * CT * lb + m + 1)
                    w_high(lb, m // 2 + 2)
                act.wait_ge(v_done, (CT - 1) * lb + 2)
                w_high(lb, QKV_CHUNKS - 1)
                act.wait_ge(v_done, (CT - 1) * lb + 4)
                copy(Kh[0][other[0], :], codes[HD:P, :])
                key_high(0, 0)
                act.wait_ge(v_dead, CT * lb + 1)
                query_copy(0, 0)
                act.wait_ge(v_dead, CT * lb + 2)
                split_v(0, 0)
                act.wait_ge(code_ready, lb + 1)
                key_high(1, 0)
                exps(0, 2 * STEPS * PAIRS * lb)
                exps(1, 2 * STEPS * PAIRS * lb + 1)
                with act.Fori(0, PAIRS - 1) as p:
                    pair(lb, p, False)
                pair(lb, PAIRS - 1, True)
                act.wait_ge(an_ready, PAIRS * lb + 5)
                attn_high(4)
                act.wait_ge(pv_done, 2 * STEPS * PAIRS * (lb + 1) + 2)
                act.wait_ge(an_ready, PAIRS * (lb + 1))
                act.wait_ge(out_taken, 2 * HEADS * (lb + 1) + 1)
                attn_high(5, slice(0, HALF))
                w_high(lb, QKV_CHUNKS + 1)
                act.wait_ge(out_taken, 2 * HEADS * (lb + 1) + 2)
                attn_high(5, slice(HALF, S))
                act.wait_ge(al_pool, 2 * (lb + 1))
                x_out(lb + 1, 0)
                act.wait_ge(al_dve, 5 * (lb + 1))
                for c in range(1, 5):
                    x_out(lb + 1, c)
                act.wait_ge(y_done, (CT - 1) * lb + 2)
                w_high(lb, QKV_CHUNKS + 2)
                x_out(lb + 1, 5)
                act.wait_ge(y_done, (CT - 1) * lb + 4)
                w_high(lb + 1, 0)
                for k in range(CT):
                    act.wait_ge(y_dead, CT * lb + k + 2)
                    x_high(lb + 1, k)

        @block.vector
        def _(dve):
            for ring, free in ((ws_ready, 2), (lo_ready, 2), (pv_done, 2), (out_taken, 2), (sum_taken, 2),
                               (y_dead, 1), (y_evac, 2), (stored, 16), (sum_stored[0], 16), (sum_stored[1], 16)):
                dve.sem_inc(ring, free)

            def max_take(e, n, j, first=False):
                dve.wait_ge(max_done, STEPS * n + j + 1)
                dve.tensor_reduce(nmax[:, e, j:j + 1], D(1) if first and j % 2 else D(2), AX_X, ALU.max, negate=True).then_inc(max_taken, 1)

            def low(u, s):
                dve.wait_ge(probs_ready, 2 * (s + 1))
                dve.wait_ge(pv_done, s + 1)
                dve.tensor_tensor(Pl[u % 2], p32[:, u % 2, :], Ph[u % 2], ALU.subtract).then_inc(lo_ready, 1)

            def query_high(e, pr):
                dve.tensor_copy(Qh[e], qa[e][:, bass.ds(pr, 1), :].rearrange("p a s -> p (a s)")).then_inc(qh_ready, 1)

            def row(e, n):
                dve.wait_ge(row_done, n + 1)
                r = first_other[e]
                dve.tensor_tensor(Q3[e][r:r + TT, :].rearrange("p (t q) -> p t q", t=TT),
                                  ps[0:TT, 4:5, 0:P].to_broadcast([TT, TT, P]),
                                  codes[0:TT, :].rearrange("p (t q) -> p t q", t=TT), ALU.mult).then_inc(row_ready, 1)

            def sum_half(e, g, s, half):
                dve.wait_ge(pv_done, s + 3)
                if half == 0:
                    dve.wait_ge(sum_stored[e], 16 * g + 16)
                r = first_other[e]
                dve.tensor_copy(sumrow[r:r + 1, half * HALF:(half + 1) * HALF], ps[r:r + 1, 6 + half, :]).then_inc(sum_taken, 1)

            def norm_half(lb, half):
                cols = slice(half * HALF, (half + 1) * HALF)
                dve.reciprocal(sumrow[own[1], cols], ps[other[1], 6 + half, :]).then_inc(sum_taken, 1)
                dve.wait_ge(sum_taken, 2 * HEADS * (lb + 1) + half + 1)
                dve.tensor_tensor(attn[own[1], PAIRS - 1, cols], ps[own[1], 6 + half, :], sumrow[own[1], cols],
                                  ALU.mult).then_inc(out_taken, 1)

            def attn_low(lb, c, count, toks=slice(None)):
                dve.wait_ge(ah_ready, 7 * lb + count)
                dve.tensor_tensor(xl[c][:, toks], attn[:, c, toks], xh[c][:, toks], ALU.subtract).then_inc(al_dve, 1)

            def recips(lb, count, cols):
                dve.wait_ge(rs_loaded, 16 * (PAIRS * lb + count))
                dve.reciprocal(rs[:, cols], rs[:, cols]).then_inc(rs_ready, 1)

            def pair(lb, p, last_pair, first_pair=False):
                g = PAIRS * lb + p
                for t in range(2 * STEPS):
                    e, u = t // STEPS, t % STEPS
                    n, s = 2 * g + e, 2 * STEPS * g + t
                    if u == ROW_AT and e == 0 and first_pair:
                        dve.wait_ge(fill_pool, 4 * lb + 1)
                    if u == ROW_AT and not (last_pair and e == 1):
                        row(1 - e, n + 1)
                    if u == ROW_AT and not last_pair:
                        dve.wait_ge(sc_done, STEPS * (n + 1))
                        query_high(e, p + 1)
                    ahead = 2 if u > ROW_AT else 1
                    if not (last_pair and e + ahead > 1):
                        for j in TAKES[u]:
                            max_take((e + ahead) % 2, n + ahead, j)
                    if u == 6 and not (last_pair and e == 1):
                        sum_half(e, (PAIRS - e) * lb + p, s - 3, 0)
                    if not (last_pair and t + AHEAD >= 2 * STEPS):
                        low((t + AHEAD) % STEPS, s + AHEAD)
                    if u == 7 and not (last_pair and e == 1):
                        sum_half(e, (PAIRS - e) * lb + p, s, 1)
                    if t == 4 and not first_pair:
                        recips(lb, p, slice(None))
                    if last_pair and t == 11:
                        recips(lb, PAIRS, slice(0, S // P))
                    if last_pair and t in (14, 15):
                        attn_low(lb, t - 12, t - 11)

            def x_stats(n, c):
                dve.wait_ge(xt_ready, CT * n + c + 1)
                for half in range(2):
                    dve.bn_stats(stats[:, c, 6 * half:6 * half + 6], xT[:, c, half * HALF:(half + 1) * HALF]).then_inc(stat_ready, 1)

            def x_aggregate(n):
                dve.wait_ge(stat_ready, 2 * CT * (n + 1))
                dve.sem_inc(gate, 1)
                for c in range(CT):
                    dve.bn_aggr(mv[:, c, :], stats[:, c, :]).then_inc(aggr_ready, 1)

            def means_in(n):
                dve.wait_ge(norm_pe, 4 * n + 1)
                dve.tensor_copy(gstat[:, 0:1], ps[0:GROUPS, 4, 0:1]).then_inc(norm_dve, 1)

            def deviations(n):
                dve.wait_ge(norm_pe, 4 * n + 2)
                dve.tensor_copy(cmean[:, :], ps[:, 5, 0:CT]).then_inc(norm_dve, 1)
                dve.wait_ge(norm_dve, 7 * n + 2)
                dve.tensor_tensor(dev[:, :], mv[:, :, 0], cmean[:, :], ALU.subtract).then_inc(norm_dve, 1)
                dve.wait_ge(norm_dve, 7 * n + 3)
                dve.tensor_tensor(dev2[:, :], dev[:, :], dev[:, :], ALU.mult).then_inc(norm_dve, 1)
                dve.wait_ge(norm_dve, 7 * n + 4)
                dve.tensor_tensor(cvar[:, :], dev2[:, :], mv[:, :, 1], ALU.add).then_inc(norm_dve, 1)

            def variances_in(n):
                dve.wait_ge(norm_pe, 4 * n + 3)
                dve.tensor_scalar(gstat[:, 1:2], ps[0:GROUPS, 6, 0:1], EPS, None, ALU.add).then_inc(norm_dve, 1)

            def normalise(n):
                dve.wait_ge(norm_pe, 4 * n + 4)
                dve.tensor_copy(crstd[:, :], ps[:, 7, 0:CT]).then_inc(norm_dve, 1)
                dve.wait_ge(norm_dve, 7 * (n + 1))
                for c in range(CT):
                    dve.tensor_scalar(xT[:, c, :], xT[:, c, :], cmean[:, c:c + 1], crstd[:, c:c + 1],
                                      ALU.subtract, ALU.mult).then_inc(xn_ready, 1)

            def x_low(n, k):
                dve.wait_ge(xh_ready, CT * n + k + 1)
                dve.tensor_tensor(xl[k], xT[:, k, :], xh[k], ALU.subtract).then_inc(xs_ready, 1)

            def y_out(lb, d):
                if d < CT - 1:
                    dve.wait_ge(y_done, (CT - 1) * lb + d + 1)
                else:
                    dve.wait_ge(y_dead, CT * (lb + 1) + 1)
                t0, cols = d % 2 * 4, slice(d // 2 * WC, (d // 2 + 1) * WC)
                out = resid[:, t0:t0 + 4, cols]
                dve.tensor_tensor(out, D(d % 2).rearrange("p (t n) -> p t n", t=4), out, ALU.add).then_inc(y_evac, 1)

            for c in range(CT):
                x_stats(0, c)
            x_aggregate(0)
            means_in(0)
            deviations(0)
            variances_in(0)
            normalise(0)
            for k in range(CT):
                x_low(0, k)
            with dve.Fori(0, LAYERS * B) as lb:
                dve.wait_ge(small, 32 * (lb + 1))
                for m in range(CT):
                    dve.wait_ge(mt_act, CT * lb + m + 1)
                    if m == 0:
                        dve.wait_ge(xs_ready, CT * (lb + 1))
                    for e in range(2):
                        dve.tensor_scalar(qa[e][own[e], m, :], D(m % 4)[own[e], :], qkb[own[e], m:m + 1], None,
                                          ALU.add).then_inc(mt_dve, 1)
                for r in range(HW):
                    dve.wait_ge(rel_done, HW * lb + r + 1)
                    rel_out(dve.tensor_copy, ps, qa[0], r, HD, False).then_inc(rel_dve, 1)
                for m in range(CT):
                    dve.wait_ge(mt_done, 2 * CT * lb + CT + m + 1)
                    dve.tensor_scalar(k32[:, m, :], D((CT + m) % 4), qkb[:, CT + m:CT + m + 1], SCALE,
                                      ALU.add, ALU.mult).then_inc(mt_dve, 1)
                dve.wait_ge(rowb_loaded, 32 * lb + 16)

                def v_out(d):
                    if d < CT - 1:
                        dve.wait_ge(v_done, (CT - 1) * lb + d + 1)
                    else:
                        dve.wait_ge(v_dead, CT * (lb + 1))
                    t0, cols = d % 2 * 4, slice(d // 2 * WC, (d // 2 + 1) * WC)
                    bias = rowb[:, cols].rearrange("p (a n) -> p a n", a=1).to_broadcast([P, 4, WC])
                    dve.tensor_tensor(v32[:, t0:t0 + 4, cols], D(V_PLACE[d]).rearrange("p (t n) -> p t n", t=4), bias,
                                      ALU.add).then_inc(v_evac, 1)

                for d in range(3):
                    v_out(d)
                dve.wait_ge(v_done, (CT - 1) * lb + 4)
                query_high(0, 0)
                v_out(3)
                n0 = HEADS * lb
                for j in range(TT):
                    max_take(0, n0, j, first=True)
                v_out(4)

                def fill(tile, value):
                    dve.memset(tile.bitcast(F32), value).then_inc(fill_dve, 1)

                dve.wait_ge(v_dead, CT * lb + 1)
                fill(Q3[0][other[0], :], 0.0)
                dve.wait_ge(fill_dve, 4 * lb + 1)
                row(0, n0)
                fill(K3[0][other[0], :], 1.0)
                dve.wait_ge(v_dead, CT * lb + 2)
                fill(V1[0][:, :, other[0]], 1.0)
                fill(V0[0][:, :, other[0]], 0.0)
                dve.wait_ge(v_dead, CT * lb + 3)
                dve.tensor_copy(Kh[1][other[1], :], codes[HD:P, :]).then_inc(code_ready, 1)
                query_high(1, 0)
                v_out(5)
                max_take(1, n0 + 1, 0)
                low(0, 2 * STEPS * PAIRS * lb)
                max_take(1, n0 + 1, 1)
                low(1, 2 * STEPS * PAIRS * lb + 1)
                pair(lb, 0, False, first_pair=True)
                with dve.Fori(0, PAIRS - 2) as i:
                    pair(lb, i + 1, False)
                pair(lb, PAIRS - 1, True)
                dve.wait_ge(pv_done, 2 * STEPS * PAIRS * (lb + 1) + 2)
                attn_low(lb, 4, 5)
                dve.wait_ge(sum_stored[0], 16 * PAIRS * (lb + 1) + 16)
                norm_half(lb, 0)
                attn_low(lb, 5, 6, slice(0, HALF))
                norm_half(lb, 1)
                n = lb + 1
                attn_low(lb, 5, 7, slice(HALF, S))
                x_stats(n, 0)
                dve.wait_ge(xb_ready, TT // 2 * (2 * lb + 1))
                y_out(lb, 0)
                for c in range(1, 4):
                    x_stats(n, c)
                dve.wait_ge(xb_ready, TT * (lb + 1))
                y_out(lb, 1)
                for c in range(4, CT):
                    x_stats(n, c)
                x_aggregate(n)
                y_out(lb, 2)
                means_in(n)
                deviations(n)
                variances_in(n)
                y_out(lb, 3)
                normalise(n)
                y_out(lb, 4)
                for k in range(CT - 1):
                    x_low(n, k)
                y_out(lb, 5)
                x_low(n, CT - 1)

        @block.gpsimd
        def _(pool):
            pool.memset(gstat[:, 3:4], -0.5).then_inc(primed, 1)
            pool.wait_ge(primed, 1)

            def w_low(lb, j):
                pool.wait_ge(wh_ready, CHUNKS * lb + j + 1)
                pool.tensor_tensor(wsplit(j % 2, 1), wraw[:, j % 2, :, :], wsplit(j % 2, 0), ALU.subtract).then_inc(ws_ready, 1)

            def split_qk(e, pr, n, v_tiles=None):
                pool.wait_ge(qh_ready, n + 1)
                pool.tensor_tensor(Ql[e], qa[e][:, bass.ds(pr, 1), :].rearrange("p a s -> p (a s)"), Qh[e],
                                   ALU.subtract).then_inc(low_ready, 1)
                pool.wait_ge(kh_ready, n + 1)
                if v_tiles is not None:
                    pool.wait_ge(v_dead, v_tiles)
                pool.wait_ge(low_ready, 2 * n + 1)
                pool.tensor_tensor(K3[e][own[e], :], k32[own[e], bass.ds(pr, 1), :].rearrange("p a s -> p (a s)"),
                                   Kh[e][own[e], :], ALU.subtract).then_inc(low_ready, 1)
                pool.wait_ge(low_ready, 2 * (n + 1))
                pool.sem_inc(gate, 1)

            def split_v(e, pr, n):
                pool.wait_ge(v1_ready, n + 1)
                pool.tensor_tensor(V0[e][:, :, own[e]], v32[:, :, bass.ds(pr * P + e * HD, HD)], V1[e][:, :, own[e]],
                                   ALU.subtract).then_inc(v0_ready, 1)

            def inverse_deviation(n):
                pool.wait_ge(norm_dve, 7 * n + 6)
                pool.tensor_tensor(gstat[:, 2:3], gstat[:, 1:2], gstat[:, 3:4], ALU.pow).then_inc(norm_pool, 1)
                pool.wait_ge(norm_pool, n + 1)
                pool.sem_inc(gate, 1)

            def fill(tile, value):
                pool.memset(tile.bitcast(F32), value).then_inc(fill_pool, 1)

            def normalise(lb, p):
                pool.wait_ge(recip_loaded, RECIPS * lb + 32 * (p + 1))
                pool.wait_ge(out_taken, 2 * HEADS * lb + 4 * (p + 1) + 2)
                tile = attn[:, bass.ds(p, 1), :].rearrange("p a s -> p (a s)")
                pool.tensor_tensor(tile, tile, recip[:, bass.ds(p, 1), :].rearrange("p a s -> p (a s)"), ALU.mult).then_inc(an_ready, 1)

            def attn_low(lb, c):
                pool.wait_ge(ah_ready, 7 * lb + c + 1)
                pool.tensor_tensor(xl[c], attn[:, c, :], xh[c], ALU.subtract).then_inc(al_pool, 1)

            def splits(lb, p, previous):
                for e in range(2):
                    n = HEADS * lb + 2 * p + e
                    split_v(1 - e, p + e, n + 1)
                    split_qk(e, p + 1, n + 2)
                    if previous is not None and e == 0:
                        normalise(lb, previous)

            w_low(0, 0)
            inverse_deviation(0)
            with pool.Fori(0, LAYERS * B) as lb:
                pool.wait_ge(y_dead, CT * lb + 1)
                pool.sem_inc(gate, 1)
                pool.memset(k32_flat, 0.0).then_inc(tab_zero, 1)
                pool.memset(sumrow[:, :], 0.0).then_inc(tab_zero, 1)
                for j in range(1, QKV_CHUNKS):
                    w_low(lb, j)
                n0 = HEADS * lb
                split_qk(0, 0, n0, CT * lb + 1)
                split_v(0, 0, n0)
                pool.wait_ge(v_dead, CT * (lb + 1))
                pool.sem_inc(gate, 1)
                fill(Q3[1][other[1], :], 0.0)
                fill(K3[1][other[1], :], 1.0)
                split_qk(1, 0, n0 + 1)
                fill(V1[1][:, :, other[1]], 1.0)
                fill(V0[1][:, :, other[1]], 0.0)
                splits(lb, 0, None)
                with pool.Fori(0, PAIRS - 2) as i:
                    splits(lb, i + 1, i)
                split_v(1, PAIRS - 1, n0 + HEADS - 1)
                for c in range(2):
                    attn_low(lb, c)
                w_low(lb, QKV_CHUNKS)
                normalise(lb, PAIRS - 2)
                pool.wait_ge(recip_loaded, RECIPS * (lb + 1))
                pool.wait_ge(out_taken, 2 * HEADS * (lb + 1))
                tile = attn[own[0], PAIRS - 1, :]
                pool.tensor_tensor(tile, tile, sumrow[own[0], :], ALU.mult).then_inc(an_ready, 1)
                pool.wait_ge(resid_loaded, 16 * (lb + 1))
                pool.wait_ge(rowb_loaded, 32 * (lb + 1))
                for t in range(TT):
                    pool.tensor_tensor(resid[:, t, :], resid[:, t, :], rowb[:, :], ALU.add).then_inc(xb_ready, 1)
                w_low(lb, QKV_CHUNKS + 1)
                w_low(lb, QKV_CHUNKS + 2)
                inverse_deviation(lb + 1)
                w_low(lb + 1, 0)


def kernel(x, L0_conv_Wqkv, L0_conv_Wproj, L0_conv_bproj, L0_conv_rel_pos_h, L0_conv_rel_pos_w,
           L1_conv_qkv_w, L1_conv_qkv_b, L1_conv_proj_w, L1_conv_proj_b, L1_conv_rel_pos_h, L1_conv_rel_pos_w):
    import numpy as np
    import concourse.bacc as bacc
    from concourse.bass_utils import run_bass_kernel_spmd

    def f(a):
        return np.asarray(a)

    rel = np.zeros((LAYERS, P, 2, OFFS), np.float32)
    for l, (rh, rw) in enumerate(((L0_conv_rel_pos_h, L0_conv_rel_pos_w), (L1_conv_rel_pos_h, L1_conv_rel_pos_w))):
        for i, table in enumerate((rh, rw)):
            t = f(table)[:OFFS][::-1].T
            rel[l, :HD, i] = rel[l, HD:, i] = t
    qkv_b = np.stack([np.zeros(3 * C, np.float32), f(L1_conv_qkv_b)])
    tok = np.arange(S)
    code = np.zeros((P, S), np.float32)
    code[:TT] = np.arange(TT)[:, None] == tok // P
    code[HD:] = np.concatenate([np.arange(HW)[:, None] == tok // HW, np.arange(HW)[:, None] == tok % HW])
    group = np.arange(C) // (C // GROUPS)
    member = (group[:, None] == np.arange(GROUPS)).astype(np.float32)
    arrays = {
        "x": f(x).reshape(B, S, C),
        "wqkv": np.stack([f(L0_conv_Wqkv), f(L1_conv_qkv_w)]),
        "wproj": np.stack([f(L0_conv_Wproj), f(L1_conv_proj_w)]),
        "qk_bias": np.ascontiguousarray(qkv_b[:, :2 * C].reshape(LAYERS, 2 * CT, P).transpose(0, 2, 1)),
        "v_bias": np.ascontiguousarray(qkv_b[:, 2 * C:]),
        "proj_bias": np.stack([f(L0_conv_bproj), f(L1_conv_proj_b)]),
        "rel": rel,
        "code": code,
        "ident": np.eye(P, dtype=np.float32),
        "member": np.ascontiguousarray(member.reshape(CT, P, GROUPS).transpose(1, 0, 2)) / np.float32(C // GROUPS),
        "member_t": np.ascontiguousarray(member.T.reshape(GROUPS, CT, P)),
    }
    nc = bacc.Bacc("TRN2", target_bir_lowering=False, num_devices=1)
    ins = [nc.dram_tensor(f"in_{k}", a.shape, mybir.dt.from_np(a.dtype), kind="ExternalInput").ap() for k, a in arrays.items()]
    out = nc.dram_tensor("state", ((LAYERS + 1) * B, S, C), F32, kind="ExternalOutput").ap()
    two_layers(nc, *ins, out)
    r = run_bass_kernel_spmd(nc, [{f"in_{k}": a for k, a in arrays.items()}], core_ids=[0])
    return r.results[0]["state"][LAYERS * B:].reshape(B, HW, HW, C)
```
